# Optimizing a Trainium2 kernel written in Bass

```python
import numpy as np
import jax
import jax.numpy as jnp

def _softmax(x, axis=-1):
    return jax.nn.softmax(x, axis=axis)

def _gelu(x):
    return jax.nn.gelu(x, approximate=True)

def _silu(x):
    return jax.nn.silu(x)

def _sigmoid(x):
    return jax.nn.sigmoid(x)

def _layernorm(x, axis=-1, eps=1e-05):
    m = jnp.mean(x, axis=axis, keepdims=True)
    v = jnp.var(x, axis=axis, keepdims=True)
    return (x - m) / jnp.sqrt(v + eps)

def _scatter_add(tgt, idx, src, axis=0):
    return tgt.at[idx].add(src)

def _segment_sum(src, seg, n):
    return jax.ops.segment_sum(src, seg, n)
kernel_name = 'mk_seq_postln_d1_jaxref_r4_0c1eed'

def setup_inputs(seed: int=0):
    np.random.seed(seed)
    _w = jnp.asarray

    def _L0_attn_setup():
        import jax, jax.numpy as jnp
        import numpy as np
        B, T, D = (8, 1024, 256)
        LN_EPS = 1e-05

        def _diagonal_ssm_layer(x, Wd, bd, Wi, bi, gamma, beta):
            decays = jax.nn.sigmoid(jnp.einsum('btd,de->bte', x, Wd) + bd)
            inj = jnp.einsum('btd,de->bte', x, Wi) + bi

            def step(h, di):
                d, i = di
                h = d * h + i
                return (h, h)
            h0 = jnp.zeros((x.shape[0], x.shape[2]), dtype=x.dtype)
            _, states = jax.lax.scan(step, h0, (decays.transpose(1, 0, 2), inj.transpose(1, 0, 2)))
            states = states.transpose(1, 0, 2)
            mean = jnp.mean(states, axis=-1, keepdims=True)
            var = jnp.var(states, axis=-1, keepdims=True)
            normed = (states - mean) * jax.lax.rsqrt(var + LN_EPS) * gamma + beta
            return normed + x
        key = jax.random.key(seed)
        k0, k1, k2 = jax.random.split(key, 3)
        scale = 0.02
        x = jax.random.normal(k0, (B, T, D), dtype=jnp.float32)
        Wd = jax.random.normal(k1, (D, D), dtype=jnp.float32) * scale
        bd = jnp.full((D,), 1.4, dtype=jnp.float32)
        Wi = jax.random.normal(k2, (D, D), dtype=jnp.float32) * scale
        bi = jnp.zeros((D,), dtype=jnp.float32)
        gamma = jnp.ones((D,), dtype=jnp.float32)
        beta = jnp.zeros((D,), dtype=jnp.float32)
        return {'x': x, 'Wd': Wd, 'bd': bd, 'Wi': Wi, 'bi': bi, 'gamma': gamma, 'beta': beta}
    _L0_attn_in = _L0_attn_setup()

    def _L0_ffn_setup():
        import jax, jax.numpy as jnp
        import numpy as np
        E, K = (8, 4)
        B, S, D = (4, 256, 256)
        H = D * 2 * 4 // 3

        def _swiglu(u, w1, w2, w3):
            h = jnp.einsum('...d,hd->...h', u, w1)
            v = jnp.einsum('...d,hd->...h', u, w2)
            return jnp.einsum('...h,dh->...d', jax.nn.sigmoid(h) * h * v, w3)
        key = jax.random.key(seed)
        ks = jax.random.split(key, 9)
        std = 0.02
        return {'x': jax.random.normal(ks[0], (B, S, D), jnp.float32), 'Wg': jax.random.normal(ks[1], (E, D), jnp.float32) * std, 'routing_bias': jnp.zeros((E,), jnp.float32), 'W1': jax.random.normal(ks[2], (E, H, D), jnp.float32) * std, 'W2': jax.random.normal(ks[3], (E, H, D), jnp.float32) * std, 'W3': jax.random.normal(ks[4], (E, D, H), jnp.float32) * std, 'Ws1': jax.random.normal(ks[5], (H, D), jnp.float32) * std, 'Ws2': jax.random.normal(ks[6], (H, D), jnp.float32) * std, 'Ws3': jax.random.normal(ks[7], (D, H), jnp.float32) * std}
    _L0_ffn_in = _L0_ffn_setup()
    _d = {'L0_attn_x': _L0_attn_in['x'], 'L0_attn_Wd': _L0_attn_in['Wd'], 'L0_attn_bd': _L0_attn_in['bd'], 'L0_attn_Wi': _L0_attn_in['Wi'], 'L0_attn_bi': _L0_attn_in['bi'], 'L0_attn_gamma': _L0_attn_in['gamma'], 'L0_attn_beta': _L0_attn_in['beta'], 'L0_ffn_Wg': _L0_ffn_in['Wg'], 'L0_ffn_routing_bias': _L0_ffn_in['routing_bias'], 'L0_ffn_W1': _L0_ffn_in['W1'], 'L0_ffn_W2': _L0_ffn_in['W2'], 'L0_ffn_W3': _L0_ffn_in['W3'], 'L0_ffn_Ws1': _L0_ffn_in['Ws1'], 'L0_ffn_Ws2': _L0_ffn_in['Ws2'], 'L0_ffn_Ws3': _L0_ffn_in['Ws3']}
    _x0 = _d['L0_attn_x']
    _d['L0_attn_x'] = jax.random.normal(jax.random.fold_in(jax.random.key(seed), 1), (2, 2048, 256), dtype=_x0.dtype)
    del _x0
    return _d

def reference(L0_attn_x, L0_attn_Wd, L0_attn_bd, L0_attn_Wi, L0_attn_bi, L0_attn_gamma, L0_attn_beta, L0_ffn_Wg, L0_ffn_routing_bias, L0_ffn_W1, L0_ffn_W2, L0_ffn_W3, L0_ffn_Ws1, L0_ffn_Ws2, L0_ffn_Ws3):

    def _L0_attn_ref(x, Wd, bd, Wi, bi, gamma, beta):
        import jax, jax.numpy as jnp
        import numpy as np
        B, T, D = (8, 1024, 256)
        LN_EPS = 1e-05

        def _diagonal_ssm_layer(x, Wd, bd, Wi, bi, gamma, beta):
            decays = jax.nn.sigmoid(jnp.einsum('btd,de->bte', x, Wd) + bd)
            inj = jnp.einsum('btd,de->bte', x, Wi) + bi

            def step(h, di):
                d, i = di
                h = d * h + i
                return (h, h)
            h0 = jnp.zeros((x.shape[0], x.shape[2]), dtype=x.dtype)
            _, states = jax.lax.scan(step, h0, (decays.transpose(1, 0, 2), inj.transpose(1, 0, 2)))
            states = states.transpose(1, 0, 2)
            mean = jnp.mean(states, axis=-1, keepdims=True)
            var = jnp.var(states, axis=-1, keepdims=True)
            normed = (states - mean) * jax.lax.rsqrt(var + LN_EPS) * gamma + beta
            return normed + x
        return _diagonal_ssm_layer(x, Wd, bd, Wi, bi, gamma, beta)

    def _L0_ffn_ref(x, Wg, routing_bias, W1, W2, W3, Ws1, Ws2, Ws3):
        import jax, jax.numpy as jnp
        import numpy as np
        E, K = (8, 4)
        B, S, D = (4, 256, 256)
        H = D * 2 * 4 // 3

        def _swiglu(u, w1, w2, w3):
            h = jnp.einsum('...d,hd->...h', u, w1)
            v = jnp.einsum('...d,hd->...h', u, w2)
            return jnp.einsum('...h,dh->...d', jax.nn.sigmoid(h) * h * v, w3)
        gate = jnp.einsum('bsd,ed->bse', x, Wg) + routing_bias
        _, top_idx = jax.lax.top_k(gate, K)
        mask = jax.nn.one_hot(top_idx, E, dtype=gate.dtype).sum(-2)
        masked_gate = jnp.where(mask > 0, gate, -jnp.inf)
        probs = jax.nn.softmax(masked_gate, axis=-1)
        weights = probs * mask
        out = _swiglu(x, Ws1, Ws2, Ws3)
        h1 = jnp.einsum('bsd,ehd->ebsh', x, W1)
        h2 = jnp.einsum('bsd,ehd->ebsh', x, W2)
        eo = jnp.einsum('ebsh,edh->ebsd', jax.nn.sigmoid(h1) * h1 * h2, W3)
        out = out + jnp.einsum('ebsd,bse->bsd', eo, weights)
        return out
    x = L0_attn_x
    x = _layernorm(x + _L0_attn_ref(x, L0_attn_Wd, L0_attn_bd, L0_attn_Wi, L0_attn_bi, L0_attn_gamma, L0_attn_beta), axis=-1)
    x = _layernorm(x + _L0_ffn_ref(x, L0_ffn_Wg, L0_ffn_routing_bias, L0_ffn_W1, L0_ffn_W2, L0_ffn_W3, L0_ffn_Ws1, L0_ffn_Ws2, L0_ffn_Ws3), axis=-1)
    return x

_drawn_inputs = setup_inputs


def setup_inputs(seed=0):
    import zlib

    import numpy as np

    out = dict(_drawn_inputs(seed))
    spreads = {'L0_attn_bd': (1.399999976158142, 0.2),
     'L0_attn_bi': (0.0, 0.1),
     'L0_attn_gamma': (1.0, 0.2),
     'L0_attn_beta': (0.0, 0.1),
     'L0_ffn_routing_bias': (0.0, 0.8)}
    factors = {'L0_ffn_Wg': 5.618,
     'L0_ffn_W1': 4.065,
     'L0_ffn_W2': 3.999,
     'L0_ffn_W3': 4.004,
     'L0_ffn_Ws1': 3.615,
     'L0_ffn_Ws2': 3.563,
     'L0_ffn_Ws3': 3.561}
    for name, (base, spread) in spreads.items():
        noise = np.random.default_rng([zlib.crc32(name.encode()), seed]).standard_normal(out[name].shape)
        drawn = base * np.exp(spread * noise) if base else spread * noise
        out[name] = jnp.asarray(drawn.astype(out[name].dtype))
    for name, factor in factors.items():
        out[name] = (out[name] * factor).astype(out[name].dtype)
    return out
```

```python
from contextlib import ExitStack

import numpy as np
import concourse.bass as bass
from concourse import mybir

P = 128
ALU = mybir.AluOpType
ACT = mybir.ActivationFunctionType
F32 = mybir.dt.float32
F16 = mybir.dt.float16
U32 = mybir.dt.uint32
AX_X = mybir.AxisListType.X
LN_EPS = 1e-5

TT = 512
JT = TT // P
TB = 256
JB = TB // P
XS = 16.0
WS = 64.0


def dims(H, D):
    full = H // P
    rem = H - full * P
    return full, rem, D // P


class Tally:

    def __init__(self, eng, sem, per_turn=0, turn=0, base=0):
        self.eng, self.sem, self.base, self.n = eng, sem, base + turn * per_turn, 0

    def add(self, ins):
        self.n += 1
        return ins.then_inc(self.sem, 1)

    def wait(self):
        self.eng.wait_ge(self.sem, self.base + self.n)


def build(nc, xT, x_tok, small, wpack, out):
    E1 = wpack.shape[0]
    E = E1 - 1
    K = 4
    N, D = x_tok.shape
    B = 2
    H = 682
    FC, REM, KD = dims(H, D)
    NC = FC + 1
    NT = N // P
    NI = N // B // TT
    NBLK = N // TB
    MW = KD * (2 * FC + 1) * P
    DW = NC * D
    HVS = 4
    SLOTS = 3
    R2 = 64
    OG, OB, OR, OC, OGW = 0, D, 2 * D, 2 * D + E, 2 * D + E + 4
    OW = OGW + KD * E
    SM = OW + 2 * KD * D
    assert small.shape[1] == SM and KD == 2 and B == 2

    ctx = ExitStack()
    with ctx:
        def sb(name, shape, dt):
            return ctx.enter_context(nc.sbuf_tensor(name, shape, dt))

        def sem(name):
            return ctx.enter_context(nc.semaphore(name))

        sm = sb("sm", [P, SM], F32)
        ident = sb("ident", [P, P], F32)
        y = sb("y", [P, NT, D], F32)
        y_hi = sb("y_hi", [P, KD, N], F16)
        y_lo = sb("y_lo", [P, KD, N], F16)
        half_bd = sb("half_bd", [P, 2], F32)
        gw_hi = sb("gw_hi", [P, KD, E], F16)
        gw_lo = sb("gw_lo", [P, KD, E], F16)
        neg_half = sb("neg_half", [P, JT], F32)
        carry = sb("carry", [P, B, KD], F32)
        xt = [sb(f"xt{b}", [P, KD, TT], F32) for b in range(B)]
        u = [sb(f"u{b}", [P, JT, D], F32) for b in range(B)]
        dec = [sb(f"dec{b}", [P, KD, TT], F32) for b in range(B)]
        inj = [sb(f"inj{b}", [P, KD, TT], F32) for b in range(B)]
        st = [sb(f"st{b}", [P, KD, TT], F32) for b in range(B)]
        zr = sb("zr", [P, JT, D], F32)
        yb = [sb(f"yb{b}", [P, JT, D], F32) for b in range(B)]
        stat = sb("stat", [P, JT, 6], F32)
        mv1 = sb("mv1", [P, JT, 2], F32)
        mv2 = sb("mv2", [P, JT, 2], F32)
        ve1 = sb("ve1", [P, JT], F32)
        ve2 = sb("ve2", [P, JT], F32)
        rs1 = sb("rs1", [P, JT], F32)
        rs2 = sb("rs2", [P, JT], F32)
        gate = sb("gate", [P, NT, E], F32)
        top = sb("top", [P, NT, 8], F32)
        topi = sb("topi", [P, NT, 8], U32)
        topf = sb("topf", [P, NT, K], F32)
        e4 = sb("e4", [P, NT, K], F32)
        es = sb("es", [P, NT], F32)
        iota = sb("iota", [P, E], F32)
        hot = sb("hot", [P, NT, E], F32)
        wd = sb("wd", [P, NT, E1], F32)
        stage = sb("stage", [P, MW + DW], F32)
        wa = [sb(f"wa{s}", [P, 2, MW], F16) for s in range(2)]
        w3 = [sb(f"w3{s}", [P, 2, DW], F16) for s in range(2)]
        xb = sb("xb", [P, 2, KD, TB], F16)
        sil = sb("sil", [P, SLOTS, TB], F32)
        g32 = sb("g32", [P, SLOTS, TB], F32)
        g_hi = sb("g_hi", [P, NC, TB], F16)
        g_lo = sb("g_lo", [P, FC, TB], F16)
        ob = sb("ob", [P, JT, D], F32)

        psA = ctx.enter_context(nc.psum_tensor("psA", [P, 4, 512], F32))
        psB = ctx.enter_context(nc.psum_tensor("psB", [P, 2, 512], F32))
        psC = ctx.enter_context(nc.psum_tensor("psC", [P, 2, 512], F32))

        s_small = sem("s_small")
        s_passed = sem("s_passed")
        s_xt = [sem(f"s_xt{b}") for b in range(B)]
        s_xtok = [sem(f"s_xtok{b}") for b in range(B)]
        s_stage = sem("s_stage")
        s_out = sem("s_out")
        s_id = sem("s_id")
        s_pool = sem("s_pool")
        s_pool2 = sem("s_pool2")
        s_const = sem("s_const")
        s_halfbd = sem("s_halfbd")
        s_gwh = sem("s_gwh")
        s_mm = sem("s_mm")
        s_mmfree = sem("s_mmfree")
        s_act = sem("s_act")
        s_dve = sem("s_dve")
        s_scan = sem("s_scan")
        s_st = sem("s_st")
        s_zfree = sem("s_zfree")
        s_mv1 = sem("s_mv1")
        s_mv2 = sem("s_mv2")
        s_rs1 = sem("s_rs1")
        s_rs2 = sem("s_rs2")
        s_u = sem("s_u")
        s_r = sem("s_r")
        s_yb = sem("s_yb")
        s_ycopy = sem("s_ycopy")
        s_yt = sem("s_yt")
        s_yhi = sem("s_yhi")
        s_ylo = sem("s_ylo")
        s_gate = sem("s_gate")
        s_e4 = sem("s_e4")
        s_exp = sem("s_exp")
        s_dve2 = sem("s_dve2")
        s_wset = sem("s_wset")
        s_stfree = sem("s_stfree")
        s_x = sem("s_x")
        s_hv = sem("s_hv")
        s_sil = sem("s_sil")
        s_g32 = sem("s_g32")
        s_ghi = sem("s_ghi")
        s_g = sem("s_g")
        s_w3 = sem("s_w3")
        s_of = sem("s_of")
        s_mvD = sem("s_mvD")
        s_rsD = sem("s_rsD")
        s_ob = sem("s_ob")
        s_dveD = sem("s_dveD")

        block = ctx.enter_context(nc.Block())

        gamma = sm[:, OG:OG + D]
        beta = sm[:, OB:OB + D]
        rb = sm[:, OR:OR + E]
        bi = sm[:, OC + 2:OC + 4]
        wg = sm[:, OGW:OGW + KD * E]
        wdi = sm[:, OW:OW + 2 * KD * D].rearrange("p (w k e) -> p w k e", w=2, k=KD)

        def tok(i, b):
            return b * (N // B) + i * TT

        def counted(eng, sem_, value):
            eng.wait_ge(sem_, value)
            eng.sem_inc(s_passed, 1)

        @block.sync
        def _(sp):
            sp.dma_start(sm[:, :], small).then_inc(s_small, 16)

            def load_turn(i):
                for b in range(B):
                    s = 2 * i + b
                    n0 = tok(i, b)
                    if not isinstance(i, int):
                        sp.wait_ge(s_mm, 4 * s - 4)
                    sp.dma_start(xt[b][:, :, :], xT[:, :, bass.ds(n0, TT)]).then_inc(s_xt[b], 16)
                    if not isinstance(i, int):
                        sp.wait_ge(s_r, s - 1)
                    sp.dma_start(u[b][:, :, :], x_tok[bass.ds(n0, TT), :].rearrange("(j p) d -> p j d", p=P))\
                        .then_inc(s_xtok[b], 16)

            load_turn(0)
            sp.dma_start(stage[:, :], wpack[0]).then_inc(s_stage, 16)
            with sp.Fori(1, NI) as i:
                load_turn(i)
            with sp.Fori(1, E1) as e:
                sp.wait_ge(s_stfree, e)
                sp.dma_start(stage[:, :], wpack[bass.ds(e, 1), :, :].rearrange("a p n -> p (a n)")).then_inc(s_stage, 16)
            with sp.Fori(0, NT // JT) as t:
                sp.wait_ge(s_ob, t + 1)
                sp.dma_start(out[bass.ds(t * TT, TT), :].rearrange("(j p) d -> p j d", p=P), ob[:, :, :])\
                    .then_inc(s_out, 16)
            sp.wait_ge(s_out, 16 * (NT // JT))

        @block.gpsimd
        def _(pool):
            pool.memset(ident[:, :], 0.0).then_inc(s_id, 1)
            pool.wait_ge(s_id, 1)
            pool.affine_select(out=ident[:, :], in_=ident[:, :], compare_op=ALU.not_equal, fill=1.0, base=0,
                               pattern=[[-1, P]], channel_multiplier=1).then_inc(s_const, 1)
            pool.memset(neg_half[:, :], -0.5).then_inc(s_const, 1)
            pool.memset(carry[:, :, :], 0.0).then_inc(s_const, 1)
            pool.memset(g_hi[:, :, :], 0.0).then_inc(s_const, 1)
            pool.memset(w3[0][:, :, :], 0.0).then_inc(s_const, 1)
            pool.memset(w3[1][:, :, :], 0.0).then_inc(s_const, 1)
            pool.iota(iota[:, :], pattern=[[1, E]], base=0, channel_multiplier=0,
                      allow_small_or_imprecise_dtypes=True).then_inc(s_const, 1)
            pool.sem_inc(s_of, 1)
            pool.sem_inc(s_g32, HVS)
            pool.sem_inc(s_g, SLOTS)
            pool.wait_ge(s_small, 16)
            pool.wait_ge(s_const, 7)

            def rstd(mv, ve, rs, mv_sem, mv_value, rs_sem, t):
                counted(pool, mv_sem, mv_value)
                t.add(pool.tensor_scalar(ve[:, :], mv[:, :, 1], 1.0, LN_EPS, ALU.mult, ALU.add))
                t.wait()
                pool.tensor_tensor(rs[:, :], ve[:, :], neg_half[:, :], ALU.pow).then_inc(rs_sem, 1)

            with pool.Fori(0, NI) as i:
                t = Tally(pool, s_pool, 6, i)
                for b in range(B):
                    counted(pool, s_xtok[b], 16 * i + 16)
                    t.add(pool.tensor_scalar(u[b][:, :, :], u[b][:, :, :], 2.0, 1.0, ALU.mult, ALU.mult))
                    t.wait()
                    pool.tensor_tensor(u[b][:, :, :], u[b][:, :, :],
                                       beta.unsqueeze(1).to_broadcast([P, JT, D]), ALU.add).then_inc(s_u, 1)
                for b in range(B):
                    s = 2 * i + b
                    rstd(mv1, ve1, rs1, s_mv1, s + 1, s_rs1, t)
                    rstd(mv2, ve2, rs2, s_mv2, s + 1, s_rs2, t)
                assert t.n == 6

            MP = MW // 4
            pieces = [(a * MP, MP) for a in range(4)]

            def convert(n, w):
                counted(pool, s_stage, 16 * n + 16)
                if not isinstance(n, int) or n >= 2:
                    counted(pool, s_w3, (n - 1) * NBLK)
                t = Tally(pool, s_pool2, 12, n)
                for a, m in pieces + [(MW, DW)]:
                    hi = wa[w][:, 0, a:a + m] if a < MW else w3[w][:, 0, :]
                    t.add(pool.tensor_scalar(hi, stage[:, a:a + m], WS, 1.0, ALU.mult, ALU.mult))
                    t.add(pool.tensor_scalar(stage[:, a:a + m], stage[:, a:a + m], WS, 1.0, ALU.mult, ALU.mult))
                t.wait()
                for a, m in pieces:
                    pool.tensor_tensor(wa[w][:, 1, a:a + m], stage[:, a:a + m], wa[w][:, 0, a:a + m], ALU.subtract)
                a, m = MW, FC * D
                t.add(pool.tensor_tensor(w3[w][:, 1, 0:m], stage[:, a:a + m], w3[w][:, 0, 0:m], ALU.subtract))
                t.add(pool.tensor_tensor(w3[w][0:R2, 1, m:DW], stage[0:R2, a + m:a + DW], w3[w][0:R2, 0, m:DW],
                                         ALU.subtract))
                t.wait()
                assert t.n == 12
                pool.sem_inc(s_wset, 1)
                pool.sem_inc(s_stfree, 1)

            convert(0, 0)
            convert(1, 1)
            with pool.Fori(1, E1 // 2) as p:
                convert(2 * p, 0)
                convert(2 * p + 1, 1)
            convert(E1 - 1, 0)

            with pool.Fori(0, NT // JT) as i:
                t = Tally(pool, s_pool, 1, i, 6 * NI)
                rstd(mv1, ve1, rs1, s_mvD, i + 1, s_rsD, t)

        @block.scalar
        def _(act):
            act.wait_ge(s_halfbd, 1)

            def acts(i, b):
                s = 2 * i + b
                if not isinstance(i, int):
                    act.wait_ge(s_scan, 2 * s - 2)
                for m in range(KD):
                    act.wait_ge(s_mm, 4 * s + 2 * m + 1)
                    act.activation(dec[b][:, m, :], psA[:, 2 * m, :], ACT.Tanh, bias=half_bd[:, m:m + 1], scale=0.5)\
                        .then_inc(s_mmfree, 1)
                    act.wait_ge(s_mm, 4 * s + 2 * m + 2)
                    act.activation(inj[b][:, m, :], psA[:, 2 * m + 1, :], ACT.Identity, bias=bi[:, m:m + 1])\
                        .then_inc(s_mmfree, 1)

            def high(i, b):
                s = 2 * i + b
                n0 = tok(i, b)
                act.wait_ge(s_yt, s + 1)
                act.activation(y_hi[:, :, bass.ds(n0, TT)], psC[:, :, :], ACT.Copy, scale=XS).then_inc(s_yhi, 1)
                act.activation(y[:, bass.ds(b * (NT // B) + i * JT, JT), :], yb[b][:, :, :], ACT.Copy)\
                    .then_inc(s_ycopy, 1)

            acts(0, 0)
            acts(0, 1)
            with act.Fori(1, NI) as i:
                acts(i, 0)
                high(i - 1, 0)
                acts(i, 1)
                high(i - 1, 1)
            high(NI - 1, 0)
            high(NI - 1, 1)

            act.wait_ge(s_e4, 1)
            act.activation(e4[:, :, :], e4[:, :, :], ACT.Exp).then_inc(s_exp, 1)

            def ffn_block(g):
                def silu(c):
                    act.wait_ge(s_hv, NC * g + c + 1)
                    act.wait_ge(s_g32, NC * g + c + 1 - SLOTS + HVS)
                    rows = P if c < FC else REM
                    act.activation(sil[0:rows, c % SLOTS, :] if c < FC else sil[R2:R2 + rows, c % SLOTS, :],
                                   psA[0:rows, c % HVS, 0:TB], ACT.Silu, scale=1.0 / (XS * WS)).then_inc(s_sil, 1)

                def high(c):
                    act.wait_ge(s_g32, NC * g + c + 1 + HVS)
                    rows = P if c < FC else REM
                    act.activation(g_hi[0:rows, c, :], g32[0:rows, c % SLOTS, :], ACT.Copy).then_inc(s_ghi, 1)

                for c in range(NC):
                    silu(c)
                    if c:
                        high(c - 1)
                high(NC - 1)

            act.wait_ge(s_halfbd, 1)
            act.activation(sil[:, 0, 0:2], half_bd[:, :], ACT.Silu).then_inc(s_act, 1)
            act.wait_ge(s_act, 1)
            with act.Fori(0, E1) as e:
                with act.Fori(0, NBLK) as i:
                    ffn_block(e * NBLK + i)

        @block.tensor
        def _(pe):
            pe.wait_ge(s_small, 16)
            pe.wait_ge(s_const, 7)

            def products(i, b):
                s = 2 * i + b
                pe.wait_ge(s_xt[b], 16 * i + 16)
                for m in range(KD):
                    for w in range(2):
                        q = 2 * m + w
                        if not (isinstance(s, int) and s == 0):
                            pe.wait_ge(s_mmfree, 4 * s + q - 3)
                        for k in range(KD):
                            last = pe.matmul(psA[:, q, :], wdi[:, w, k, m * P:(m + 1) * P], xt[b][:, k, :],
                                             start=(k == 0), stop=(k == KD - 1))
                        last.then_inc(s_mm, 1)

            def states(i, b):
                s = 2 * i + b
                pe.wait_ge(s_scan, 2 * s + 2)
                for h in range(2):
                    if not (isinstance(s, int) and s == 0):
                        pe.wait_ge(s_zfree, 2 * s + h - 1)
                    for j in range(2):
                        for m in range(KD):
                            t0 = (2 * h + j) * P
                            last = pe.transpose(psB[:, h, j * D + m * P:j * D + (m + 1) * P],
                                                st[b][:, m, t0:t0 + P], ident[:, :])
                    last.then_inc(s_st, 1)

            def y_turn(i, b):
                s = 2 * i + b
                pe.wait_ge(s_yb, s + 1)
                if not (isinstance(s, int) and s == 0):
                    pe.wait_ge(s_ylo, s)
                for k in range(KD):
                    for j in range(JT):
                        last = pe.transpose(psC[:, k, j * P:(j + 1) * P], yb[b][:, j, k * P:(k + 1) * P], ident[:, :])
                last.then_inc(s_yt, 1)

            products(0, 0)
            products(0, 1)
            states(0, 0)
            states(0, 1)
            with pe.Fori(1, NI) as i:
                products(i, 0)
                y_turn(i - 1, 0)
                products(i, 1)
                y_turn(i - 1, 1)
                states(i, 0)
                states(i, 1)
            y_turn(NI - 1, 0)
            y_turn(NI - 1, 1)

            pe.wait_ge(s_ylo, 2 * NI)
            pe.wait_ge(s_gwh, 2)
            with pe.Fori(0, NT) as t:
                parts = [(y_hi, gw_hi), (y_hi, gw_lo), (y_lo, gw_hi)]
                for n, (a, w) in enumerate(parts):
                    for k in range(KD):
                        last = pe.matmul(psC[:, 0, bass.ds(t * E, E)], a[:, k, bass.ds(t * P, P)], w[:, k, :],
                                         start=(n == 0 and k == 0), stop=(n == 2 and k == KD - 1))
                last.then_inc(s_gate, 1)

            def ffn_block(w, g):
                pe.wait_ge(s_x, g + 1)
                W = wa[w][:, :, :].rearrange("p s (k c n) -> p s k c n", k=KD, n=P)
                W3 = w3[w][:, :, :].rearrange("p s (c d) -> p s c d", d=D)

                def side(dst, ci):
                    for k in range(KD):
                        for n, (ws, xs) in enumerate([(0, 0), (0, 1), (1, 0)]):
                            last = pe.matmul(dst, W[:, ws, k, ci, :], xb[:, xs, k, :],
                                             start=(k == 0 and n == 0), stop=(k == KD - 1 and n == 2))
                    return last

                for c in range(NC):
                    before = c - 4 if c >= 4 else (c + 4 if c + 4 < NC else c) - NC
                    pe.wait_ge(s_g32, NC * g + before + 1 + HVS)
                    last = side(psA[:, c % HVS, 0:TB], 2 * c)
                    if c < FC:
                        last = side(psA[:, c % HVS, TB:2 * TB], 2 * c + 1)
                    last.then_inc(s_hv, 1)
                pe.wait_ge(s_of, g + 1)
                for c in range(NC):
                    pe.wait_ge(s_g, NC * g + c + 1 + SLOTS)
                    for j in range(JB):
                        o = psB[:, j, 0:D]
                        if c < FC:
                            for n, (a, ws) in enumerate([(g_hi, 0), (g_hi, 1), (g_lo, 0)]):
                                pe.matmul(o, a[:, c, j * P:(j + 1) * P], W3[:, ws, c, :],
                                          start=(c == 0 and n == 0), stop=False)
                        else:
                            r = R2 + REM
                            for ws in range(2):
                                last = pe.matmul(o, g_hi[0:r, c, j * P:(j + 1) * P], W3[0:r, ws, c, :],
                                                 start=False, stop=(ws == 1))
                last.then_inc(s_w3, 1)

            def expert(n, w):
                counted(pe, s_wset, n + 1)
                with pe.Fori(0, NBLK) as i:
                    ffn_block(w, n * NBLK + i)

            with pe.Fori(0, E1 // 2) as p:
                expert(2 * p, 0)
                expert(2 * p + 1, 1)
            expert(E1 - 1, 0)

        @block.vector
        def _(dve):
            dve.wait_ge(s_small, 16)
            dve.wait_ge(s_const, 7)
            dve.tensor_scalar(half_bd[:, :], sm[:, OC:OC + 2], 0.5, None, ALU.mult).then_inc(s_halfbd, 1)
            dve.tensor_scalar(gw_hi[:, :, :].rearrange("p k e -> p (k e)"), wg, WS, None, ALU.mult).then_inc(s_gwh, 1)
            dve.wait_ge(s_gwh, 1)
            dve.scalar_tensor_tensor(gw_lo[:, :, :].rearrange("p k e -> p (k e)"), wg, WS,
                                     gw_hi[:, :, :].rearrange("p k e -> p (k e)"), ALU.mult, ALU.subtract)\
                .then_inc(s_gwh, 1)

            PER = 16

            def scans(i, b, t):
                s = 2 * i + b
                dve.wait_ge(s_mmfree, 4 * s + 4)
                t.add(dve.tensor_scalar(dec[b][:, :, :], dec[b][:, :, :], 0.5, 0.5, ALU.mult, ALU.add))
                t.wait()
                if not isinstance(i, int):
                    dve.wait_ge(s_st, 2 * s - 2)
                for m in range(KD):
                    dve.tensor_tensor_scan(st[b][:, m, :], dec[b][:, m, :], inj[b][:, m, :], carry[:, b, m:m + 1],
                                           ALU.mult, ALU.add).then_inc(s_scan, 1)
                dve.wait_ge(s_scan, 2 * s + 2)
                t.add(dve.tensor_copy(carry[:, b, :], st[b][:, :, TT - 1]))

            def norms(i, b, t):
                s = 2 * i + b
                for j in range(JT):
                    if j % 2 == 0:
                        dve.wait_ge(s_st, 2 * s + j // 2 + 1)
                    ins = dve.bn_stats(stat[:, j, :], psB[:, j // 2, (j % 2) * D:(j % 2 + 1) * D])
                t.add(ins)
                t.wait()
                dve.sem_inc(s_passed, 1)
                for j in range(JT):
                    ins = dve.bn_aggr(mv1[:, j, :], stat[:, j, :])
                ins.then_inc(s_mv1, 1)
                dve.wait_ge(s_mv1, s + 1)
                for j in range(JT):
                    ins = dve.scalar_tensor_tensor(zr[:, j, :], psB[:, j // 2, (j % 2) * D:(j % 2 + 1) * D],
                                                   mv1[:, j, 0:1], gamma, ALU.subtract, ALU.mult)
                    if j % 2:
                        ins.then_inc(s_zfree, 1)
                dve.wait_ge(s_zfree, 2 * s + 2)
                dve.wait_ge(s_rs1, s + 1)
                dve.wait_ge(s_u, s + 1)
                for j in range(JT):
                    ins = dve.scalar_tensor_tensor(zr[:, j, :], zr[:, j, :], rs1[:, j:j + 1], u[b][:, j, :],
                                                   ALU.mult, ALU.add)
                ins.then_inc(s_r, 1)
                dve.wait_ge(s_r, s + 1)
                for j in range(JT):
                    ins = dve.bn_stats(stat[:, j, :], zr[:, j, :])
                t.add(ins)
                t.wait()
                dve.sem_inc(s_passed, 1)
                for j in range(JT):
                    ins = dve.bn_aggr(mv2[:, j, :], stat[:, j, :])
                ins.then_inc(s_mv2, 1)
                dve.wait_ge(s_rs2, s + 1)
                if not isinstance(i, int):
                    dve.wait_ge(s_ycopy, s - 1)
                for j in range(JT):
                    ins = dve.tensor_scalar(yb[b][:, j, :], zr[:, j, :], mv2[:, j, 0:1], rs2[:, j:j + 1],
                                            ALU.subtract, ALU.mult)
                ins.then_inc(s_yb, 1)

            def low(i, b):
                s = 2 * i + b
                n0 = tok(i, b)
                dve.wait_ge(s_yhi, s + 1)
                for k in range(KD):
                    ins = dve.scalar_tensor_tensor(y_lo[:, k, bass.ds(n0, TT)], psC[:, k, :], XS,
                                                   y_hi[:, k, bass.ds(n0, TT)], ALU.mult, ALU.subtract)
                ins.then_inc(s_ylo, 1)

            t = Tally(dve, s_dve)
            scans(0, 0, t)
            scans(0, 1, t)
            norms(0, 0, t)
            norms(0, 1, t)
            PER = t.n
            with dve.Fori(1, NI) as i:
                t = Tally(dve, s_dve, PER, i)
                scans(i, 0, t)
                low(i - 1, 0)
                scans(i, 1, t)
                low(i - 1, 1)
                norms(i, 0, t)
                norms(i, 1, t)
                assert t.n == PER
            low(NI - 1, 0)
            low(NI - 1, 1)

            t = Tally(dve, s_dve2)
            dve.wait_ge(s_gate, NT)
            t.add(dve.scalar_tensor_tensor(gate[:, :, :], psC[:, 0, 0:NT * E].rearrange("p (t e) -> p t e", e=E),
                                           1.0 / (XS * WS), rb.unsqueeze(1).to_broadcast([P, NT, E]),
                                           ALU.mult, ALU.add))
            t.wait()
            for n in range(NT):
                ins = dve.max(top[:, n, :], gate[:, n, :])
            t.add(ins)
            t.wait()
            dve.tensor_tensor(e4[:, :, :], top[:, :, 0:K], top[:, :, 0:1].to_broadcast([P, NT, K]), ALU.subtract)\
                .then_inc(s_e4, 1)
            for n in range(NT):
                ins = dve.max_index(topi[:, n, :], top[:, n, :], gate[:, n, :])
            t.add(ins)
            t.wait()
            t.add(dve.tensor_copy(topf[:, :, :], topi[:, :, 0:K]))
            dve.wait_ge(s_exp, 1)
            t.add(dve.reduce_sum(es[:, :], e4[:, :, :], axis=AX_X))
            t.wait()
            t.add(dve.reciprocal(es[:, :], es[:, :]))
            t.wait()
            t.add(dve.scalar_tensor_tensor(e4[:, :, :], e4[:, :, :], 1.0 / WS,
                                           es[:, :].unsqueeze(2).to_broadcast([P, NT, K]), ALU.mult, ALU.mult))
            t.add(dve.memset(wd[:, :, :], 0.0))
            t.wait()
            t.add(dve.memset(wd[:, :, 0:1], 1.0 / WS))
            for k in range(K):
                t.add(dve.tensor_tensor(hot[:, :, :], iota[:, :].unsqueeze(1).to_broadcast([P, NT, E]),
                                        topf[:, :, k:k + 1].to_broadcast([P, NT, E]), ALU.is_equal))
                t.wait()
                t.add(dve.tensor_tensor(hot[:, :, :], hot[:, :, :], e4[:, :, k:k + 1].to_broadcast([P, NT, E]),
                                        ALU.mult))
                t.wait()
                t.add(dve.tensor_tensor(wd[:, :, 1:E1], wd[:, :, 1:E1], hot[:, :, :], ALU.add))
                t.wait()

            def fill(i):
                dve.tensor_copy(xb[:, 0, :, :], y_hi[:, :, bass.ds(i * TB, TB)])
                dve.tensor_copy(xb[:, 1, :, :], y_lo[:, :, bass.ds(i * TB, TB)]).then_inc(s_x, 1)

            def ffn_block(g, i, e, nxt):
                def gated(c):
                    dve.wait_ge(s_g, NC * g + c + 1)
                    dve.wait_ge(s_sil, NC * g + c + 1)
                    r0, rows = (0, P) if c < FC else (R2, REM)
                    src = psA[:, c % HVS, TB:2 * TB] if c < FC else psA[R2:R2 + REM, c % HVS, 0:TB]
                    dve.scalar_tensor_tensor(g32[0:rows, c % SLOTS, :], src, 1.0 / (XS * WS),
                                             sil[r0:r0 + rows, c % SLOTS, :], ALU.mult, ALU.mult).then_inc(s_g32, 1)

                def low(c):
                    dve.wait_ge(s_ghi, NC * g + c + 1)
                    if c < FC:
                        dst, rows = g_lo[:, c, :], P
                    else:
                        dst, rows = g_hi[R2:R2 + REM, c, :], REM
                    dve.tensor_tensor(dst, g32[0:rows, c % SLOTS, :], g_hi[0:rows, c, :], ALU.subtract).then_inc(s_g, 1)

                for c in range(NC):
                    gated(c)
                    if c:
                        low(c - 1)
                fill(nxt)
                low(NC - 1)
                dve.wait_ge(s_w3, g + 1)
                for j in range(JB):
                    T = i * JB + j
                    ins = dve.scalar_tensor_tensor(y[:, bass.ds(T, 1), :].rearrange("p a d -> p (a d)"), psB[:, j, 0:D],
                                                   wd[:, bass.ds(T, 1), bass.ds(e, 1)].rearrange("p a b -> p (a b)"),
                                                   y[:, bass.ds(T, 1), :].rearrange("p a d -> p (a d)"),
                                                   ALU.mult, ALU.add)
                ins.then_inc(s_of, 1)

            fill(0)
            with dve.Fori(0, E1) as e:
                with dve.Fori(0, NBLK - 1) as i:
                    ffn_block(e * NBLK + i, i, e, i + 1)
                ffn_block(e * NBLK + NBLK - 1, NBLK - 1, e, 0)

            with dve.Fori(0, NT // JT) as i:
                t = Tally(dve, s_dveD, 1, i)
                dve.wait_ge(s_of, E1 * NBLK + 1)
                for j in range(JT):
                    ins = dve.bn_stats(stat[:, j, :], y[:, bass.ds(i * JT + j, 1), :].rearrange("p a d -> p (a d)"))
                t.add(ins)
                t.wait()
                dve.sem_inc(s_passed, 1)
                for j in range(JT):
                    ins = dve.bn_aggr(mv1[:, j, :], stat[:, j, :])
                ins.then_inc(s_mvD, 1)
                dve.wait_ge(s_rsD, i + 1)
                dve.wait_ge(s_out, 16 * i)
                for j in range(JT):
                    ins = dve.tensor_scalar(ob[:, j, :], y[:, bass.ds(i * JT + j, 1), :].rearrange("p a d -> p (a d)"),
                                            mv1[:, j, 0:1], rs1[:, j:j + 1], ALU.subtract, ALU.mult)
                ins.then_inc(s_ob, 1)


def pack(a):
    x = np.asarray(a["L0_attn_x"])
    B, T, D = x.shape
    x_tok = np.ascontiguousarray(x.reshape(B * T, D))
    xT = np.ascontiguousarray(x_tok.T.reshape(D // P, P, B * T).transpose(1, 0, 2))

    def cols(v):
        return np.asarray(v).reshape(D // P, P).T

    def rows(m):
        m = np.asarray(m)
        return m.reshape(D // P, P, -1).transpose(1, 0, 2).reshape(P, -1)

    small = np.concatenate(
        [np.broadcast_to(np.asarray(a[f"L0_attn_{n}"])[None], (P, D)) for n in ("gamma", "beta")]
        + [np.broadcast_to(np.asarray(a["L0_ffn_routing_bias"])[None], (P, a["L0_ffn_routing_bias"].shape[0]))]
        + [cols(a["L0_attn_bd"]), cols(a["L0_attn_bi"]), rows(np.asarray(a["L0_ffn_Wg"]).T)]
        + [rows(a["L0_attn_Wd"]), rows(a["L0_attn_Wi"])], axis=1)

    W1 = np.concatenate([np.asarray(a["L0_ffn_Ws1"])[None], np.asarray(a["L0_ffn_W1"])])
    W2 = np.concatenate([np.asarray(a["L0_ffn_Ws2"])[None], np.asarray(a["L0_ffn_W2"])])
    W3 = np.concatenate([np.asarray(a["L0_ffn_Ws3"])[None], np.asarray(a["L0_ffn_W3"])])
    E1, H, _ = W1.shape
    FC, REM, KD = dims(H, D)
    up = np.zeros((E1, P, KD, 2 * FC + 1, P), W1.dtype)
    for n, w in enumerate((W1, W2)):
        wt = w.transpose(0, 2, 1).reshape(E1, KD, P, H).transpose(0, 2, 1, 3)
        up[:, :, :, n:2 * FC:2, :] = wt[..., :FC * P].reshape(E1, P, KD, FC, P)
        up[:, :, :, 2 * FC, n * 64:n * 64 + REM] = wt[..., FC * P:]
    down = np.zeros((E1, P, FC + 1, D), W3.dtype)
    w3t = W3.transpose(0, 2, 1)
    down[:, :, :FC] = w3t[:, :FC * P].reshape(E1, FC, P, D).transpose(0, 2, 1, 3)
    for n in range(2):
        down[:, n * 64:n * 64 + REM, FC] = w3t[:, FC * P:]
    wpack = np.concatenate([up.reshape(E1, P, -1), down.reshape(E1, P, -1)], axis=2)
    return {"xT": xT, "x_tok": x_tok, "small": np.ascontiguousarray(small), "wpack": np.ascontiguousarray(wpack)}


def kernel(**inputs):
    import concourse.bacc as bacc
    from concourse.bass_utils import run_bass_kernel_spmd

    arrays = pack(inputs)
    nc = bacc.Bacc("TRN2", target_bir_lowering=False, num_devices=1)
    args = [nc.dram_tensor(n, v.shape, mybir.dt.from_np(v.dtype), kind="ExternalInput").ap()
            for n, v in arrays.items()]
    out = nc.dram_tensor("out", arrays["x_tok"].shape, F32, kind="ExternalOutput").ap()
    build(nc, *args, out)
    r = run_bass_kernel_spmd(nc, [arrays], core_ids=[0])
    return r.results[0]["out"].reshape(inputs["L0_attn_x"].shape)
```

```python
from contextlib import ExitStack

import numpy as np
import concourse.bass as bass
from concourse import mybir

P = 128
ALU = mybir.AluOpType
ACT = mybir.ActivationFunctionType
F32 = mybir.dt.float32
F16 = mybir.dt.float16
U32 = mybir.dt.uint32
AX_X = mybir.AxisListType.X
I32 = mybir.dt.int32
LN_EPS = 1e-5

TT = 512
JT = TT // P
TB = 256
JB = TB // P
XS = 16.0
WS = 64.0


def dims(H, D):
    full = H // P
    rem = H - full * P
    return full, rem, D // P


class Tally:

    def __init__(self, eng, sem, per_turn=0, turn=0, base=0):
        self.eng, self.sem, self.base, self.n = eng, sem, base + turn * per_turn, 0

    def add(self, ins):
        self.n += 1
        return ins.then_inc(self.sem, 1)

    def wait(self):
        self.eng.wait_ge(self.sem, self.base + self.n)


def build(nc, xT, x_tok, small, wpack, out):
    E1 = wpack.shape[0]
    E = E1 - 1
    K = 4
    N, D = x_tok.shape
    B = 2
    H = 682
    FC, REM, KD = dims(H, D)
    NC = FC + 1
    NT = N // P
    NI = N // B // TT
    NS = N // TB
    S1 = 6
    S2 = NS - S1
    NR = K * N // TB + E
    T1 = S1 * JB
    X2 = S2 - S1
    MW = KD * (2 * FC + 1) * P
    DW = NC * D
    HVS = 4
    SLOTS = 3
    GS = 4
    R2 = 64
    BIG = 32768.0
    OG, OB, OR, OC, OGW = 0, D, 2 * D, 2 * D + E, 2 * D + E + 4
    OW = OGW + KD * E
    SM = OW + 2 * KD * D
    assert small.shape[1] == SM and KD == 2 and B == 2 and NR * TB < BIG

    xs = nc.dram_tensor("xs", [NR * TB, D], F32, kind="Internal").ap()
    eo = nc.dram_tensor("eo", [NR * TB, D], F32, kind="Internal").ap()

    ctx = ExitStack()
    with ctx:
        def sb(name, shape, dt):
            return ctx.enter_context(nc.sbuf_tensor(name, shape, dt))

        def sem(name):
            return ctx.enter_context(nc.semaphore(name))

        sm = sb("sm", [P, SM], F32)
        ident = sb("ident", [P, P], F32)
        tri = sb("tri", [P, P], F16)
        ones = sb("ones", [P, P], F16)
        zeros = sb("zeros", [P, D], F32)
        y = sb("y", [P, NT, D], F32)
        work = sb("work", [P, 13, KD * TT], F32)

        def kt(n):
            return work[:, n, :].rearrange("p (k t) -> p k t", k=KD)

        def jd(n):
            return work[:, n, :].rearrange("p (j d) -> p j d", j=JT)

        xt, u, dec, inj, st, yb = ([v(n + b) for b in range(B)]
                                   for n, v in ((0, kt), (2, jd), (4, kt), (6, kt), (8, kt), (10, jd)))
        zr = jd(12)
        acc = work[:, 0:8, :].rearrange("p n (j d) -> p (n j) d", d=D)
        hot = work[:, 8, :]
        hot2 = work[:, 9, :]
        yh = sb("yh", [P, KD, TT], F16)
        yl = sb("yl", [P, KD, TT], F16)
        half_bd = sb("half_bd", [P, 2], F32)
        gw_hi = sb("gw_hi", [P, KD, E], F16)
        gw_lo = sb("gw_lo", [P, KD, E], F16)
        neg_half = sb("neg_half", [P, JT], F32)
        carry = sb("carry", [P, B, KD], F32)
        stat = sb("stat", [P, JT, 6], F32)
        mv1 = sb("mv1", [P, JT, 2], F32)
        mv2 = sb("mv2", [P, JT, 2], F32)
        ve1 = sb("ve1", [P, JT], F32)
        ve2 = sb("ve2", [P, JT], F32)
        rs1 = sb("rs1", [P, JT], F32)
        rs2 = sb("rs2", [P, JT], F32)

        gate = sb("gate", [P, NT, E], F32)
        top = sb("top", [P, NT, 8], F32)
        topi = sb("topi", [P, NT, 8], U32)
        topf = sb("topf", [P, NT, K], F32)
        ex = sb("ex", [P, NT, E], F32)
        es = sb("es", [P, NT], F32)
        iota_e = sb("iota_e", [P, E], F32)
        iota_r = sb("iota_r", [P, JB], F32)
        mask = sb("mask", [P, NT, E], F32)
        mask_h = sb("mask_h", [P, NT, E], F16)
        seg = sb("seg", [P, E, NT], F32)
        tot = sb("tot", [P, E, NT], F32)
        inc = sb("inc", [P, E, NT], F32)
        key = sb("key", [P, NT, E], F32)
        wk = sb("wk", [P, NT, K], F32)
        place = sb("place", [P, K, NT], U32)
        one8 = sb("one8", [P, E], F32)
        cnt = sb("cnt", [P, 6, E], F32)
        cnt_i = sb("cnt_i", [P, 2, E], I32)
        blocks = sb("blocks", [P, 2, E], I32)
        pad = sb("pad", [P, E, JB], F32)
        pad2 = sb("pad2", [P, E, JB], F32)
        pad_at = sb("pad_at", [P, E, JB], U32)

        stage = sb("stage", [P, MW + DW], F32)
        wa = [sb(f"wa{s}", [P, 2, MW], F16) for s in range(3)]
        w3 = [sb(f"w3{s}", [P, 2, DW], F16) for s in range(3)]
        SH = 2
        rows = sb("rows", [P, JB, D], F32)
        xb = sb("xb", [P, 2, KD, TB], F16)
        sil = sb("sil", [P, SLOTS, TB], F32)
        g32 = sb("g32", [P, SLOTS, TB], F32)
        g_hi = sb("g_hi", [P, NC, TB], F16)
        g_lo = sb("g_lo", [P, FC, TB], F16)
        eb = sb("eb", [P, JB, D], F32)
        back = [sb(f"back{q}", [P, D], F32) for q in range(GS)]
        nv = sb("nv", [P, JB], F32)
        nr = sb("nr", [P, JB], F32)
        na = sb("na", [P, JB], F32)

        psA = ctx.enter_context(nc.psum_tensor("psA", [P, 4, 512], F32))
        psB = ctx.enter_context(nc.psum_tensor("psB", [P, 2, 512], F32))
        psC = ctx.enter_context(nc.psum_tensor("psC", [P, 2, 512], F32))
        PO = 0

        s_small = sem("s_small")
        s_passed = sem("s_passed")
        s_xt = [sem(f"s_xt{b}") for b in range(B)]
        s_xtok = [sem(f"s_xtok{b}") for b in range(B)]
        s_stage = sem("s_stage")
        s_id = sem("s_id")
        s_const = sem("s_const")
        s_pool = sem("s_pool")
        s_pool2 = sem("s_pool2")
        s_pool3 = sem("s_pool3")
        s_halfbd = sem("s_halfbd")
        s_gwh = sem("s_gwh")
        s_mm = sem("s_mm")
        s_mmfree = sem("s_mmfree")
        s_act = sem("s_act")
        s_dve = sem("s_dve")
        s_scan = sem("s_scan")
        s_st = sem("s_st")
        s_zfree = sem("s_zfree")
        s_mv1 = sem("s_mv1")
        s_mv2 = sem("s_mv2")
        s_rs1 = sem("s_rs1")
        s_rs2 = sem("s_rs2")
        s_u = sem("s_u")
        s_r = sem("s_r")
        s_yb = sem("s_yb")
        s_ycopy = sem("s_ycopy")
        s_yt = sem("s_yt")
        s_yhi = sem("s_yhi")
        s_ylo = sem("s_ylo")
        s_gate = sem("s_gate")
        s_gev = sem("s_gev")
        s_e4 = sem("s_e4")
        s_exp = sem("s_exp")
        s_route = sem("s_route")
        s_mask = sem("s_mask")
        s_rank = sem("s_rank")
        s_blocks = sem("s_blocks")
        s_place = sem("s_place")
        s_padat = sem("s_padat")
        s_wk = sem("s_wk")
        s_scat = [sem(f"s_scat{k}") for k in range(K)]
        s_pads = sem("s_pads")
        s_wset = sem("s_wset")
        s_stfree = sem("s_stfree")
        s_rows = sem("s_rows")
        s_fill = sem("s_fill")
        s_xtr = sem("s_xtr")
        s_xhi = sem("s_xhi")
        s_x = sem("s_x")
        s_hv = sem("s_hv")
        s_sil = sem("s_sil")
        s_g32 = sem("s_g32")
        s_ghi = sem("s_ghi")
        s_g = sem("s_g")
        s_w3 = sem("s_w3")
        s_of = sem("s_of")
        s_eb = sem("s_eb")
        s_eo = sem("s_eo")
        s_back = [sem(f"s_back{q}") for q in range(GS)]
        s_sum = sem("s_sum")
        s_fin = sem("s_fin")
        s_norm = sem("s_norm")
        s_out = sem("s_out")

        block = ctx.enter_context(nc.Block())

        gamma = sm[:, OG:OG + D]
        beta = sm[:, OB:OB + D]
        rb = sm[:, OR:OR + E]
        bi = sm[:, OC + 2:OC + 4]
        wg = sm[:, OGW:OGW + KD * E]
        wdi = sm[:, OW:OW + 2 * KD * D].rearrange("p (w k e) -> p w k e", w=2, k=KD)
        NCONST = 12

        def tok(i, b):
            return b * (N // B) + i * TT

        def counted(eng, sem_, value):
            eng.wait_ge(sem_, value)
            eng.sem_inc(s_passed, 1)

        def one(ap, t):
            return ap[:, bass.ds(t, 1), :].rearrange("p a d -> p (a d)")

        def block_range(eng, e):
            n = eng.value_load(blocks[0:1, 0, bass.ds(e, 1)], min_val=1, max_val=NS)
            return n, eng.value_load(blocks[0:1, 1, bass.ds(e, 1)], min_val=0, max_val=NR)

        def experts(eng, run):
            with eng.Fori(0, E // 2) as p:
                for u_ in range(2):
                    e = 2 * p + u_
                    run(e, u_, *block_range(eng, e))

        def all_blocks(eng):
            n, before = block_range(eng, E - 1)
            return eng.snap(before + n)

        @block.sync
        def _(sp):
            sp.dma_start(sm[:, :], small).then_inc(s_small, 16)

            def load_turn(i):
                for b in range(B):
                    s = 2 * i + b
                    n0 = tok(i, b)
                    if not isinstance(i, int):
                        sp.wait_ge(s_mm, 4 * s - 4)
                    sp.dma_start(xt[b][:, :, :], xT[:, :, bass.ds(n0, TT)]).then_inc(s_xt[b], 16)
                    if not isinstance(i, int):
                        sp.wait_ge(s_r, s - 1)
                    sp.dma_start(u[b][:, :, :], x_tok[bass.ds(n0, TT), :].rearrange("(j p) d -> p j d", p=P))\
                        .then_inc(s_xtok[b], 16)

            FB = NR * TB // P // NI
            fill = eo.rearrange("(i n p) d -> i p n d", i=NI, p=P)

            def fill_rows(i):
                sp.dma_start(fill[bass.ds(i, 1), :, :, :].rearrange("i p n d -> p (i n) d"),
                             zeros[:, :].unsqueeze(1).to_broadcast([P, FB, D])).then_inc(s_fill, 16)

            load_turn(0)
            sp.wait_ge(s_const, NCONST)
            fill_rows(0)
            with sp.Fori(1, NI) as i:
                load_turn(i)
                sp.wait_ge(s_fill, 16 * i)
                fill_rows(i)

            def load_shared(b, i):
                if not isinstance(b, int) or b > 0:
                    sp.wait_ge(s_xtr, b)
                sp.dma_start(rows[:, :, :], y[:, bass.ds(JB * i, JB), :]).then_inc(s_rows, 16)

            sp.wait_ge(s_ycopy, 2 * NI)
            load_shared(0, 0)
            with sp.Fori(1, S1) as i:
                load_shared(i, i)

            sp.wait_ge(s_blocks, 1)
            sp.wait_ge(s_pads, 16 * E * JB)
            for e in range(E):
                if e < K:
                    sp.wait_ge(s_scat[e], 16 * NT)
                n, before = block_range(sp, e)
                with sp.Fori(0, n) as i:
                    b = nc.s_assert_within(sp.snap(before + i), 0, NR - 1)
                    sp.wait_ge(s_xtr, S1 + b)
                    sp.dma_start(rows[:, :, :], xs[bass.ds(b * TB, TB), :].rearrange("(j p) d -> p j d", p=P))\
                        .then_inc(s_rows, 16)
            r = all_blocks(sp)
            with sp.Fori(S1, NS) as i:
                load_shared(r + i, i)

        @block.gpsimd
        def _(pool):
            pool.memset(ident[:, :], 0.0).then_inc(s_id, 1)
            pool.memset(tri[:, :], 1.0).then_inc(s_id, 1)
            pool.memset(seg[:, :, :], 1.0).then_inc(s_id, 1)
            pool.wait_ge(s_id, 3)
            pool.affine_select(out=ident[:, :], in_=ident[:, :], compare_op=ALU.not_equal, fill=1.0, base=0,
                               pattern=[[-1, P]], channel_multiplier=1).then_inc(s_const, 1)
            pool.affine_select(out=tri[:, :], in_=tri[:, :], compare_op=ALU.is_gt, fill=0.0, base=0,
                               pattern=[[1, P]], channel_multiplier=-1).then_inc(s_const, 1)
            pool.memset(seg[:, :, 0:1], 0.0).then_inc(s_const, 1)
            pool.memset(ones[:, :], 1.0).then_inc(s_const, 1)
            pool.memset(one8[:, :], 1.0).then_inc(s_const, 1)
            pool.memset(zeros[:, :], 0.0).then_inc(s_const, 1)
            pool.memset(neg_half[:, :], -0.5).then_inc(s_const, 1)
            pool.memset(carry[:, :, :], 0.0).then_inc(s_const, 1)
            pool.memset(g_hi[:, :, :], 0.0).then_inc(s_const, 1)
            for w in range(3):
                last = pool.memset(w3[w][:, :, :], 0.0)
            last.then_inc(s_const, 1)
            pool.iota(iota_e[:, :], pattern=[[1, E]], base=0, channel_multiplier=0,
                      allow_small_or_imprecise_dtypes=True).then_inc(s_const, 1)
            pool.iota(iota_r[:, :], pattern=[[P, JB]], base=0, channel_multiplier=1,
                      allow_small_or_imprecise_dtypes=True).then_inc(s_const, 1)
            pool.sem_inc(s_of, 1)
            pool.sem_inc(s_g32, HVS)
            pool.sem_inc(s_g, SLOTS)
            pool.sem_inc(s_eo, 16)
            pool.wait_ge(s_small, 16)
            pool.wait_ge(s_const, NCONST)

            def rstd(mv, ve, rs, mv_sem, mv_value, rs_sem, t):
                counted(pool, mv_sem, mv_value)
                t.add(pool.tensor_scalar(ve[:, :], mv[:, :, 1], 1.0, LN_EPS, ALU.mult, ALU.add))
                t.wait()
                pool.tensor_tensor(rs[:, :], ve[:, :], neg_half[:, :], ALU.pow).then_inc(rs_sem, 1)

            with pool.Fori(0, NI) as i:
                t = Tally(pool, s_pool, 6, i)
                for b in range(B):
                    counted(pool, s_xtok[b], 16 * i + 16)
                    t.add(pool.tensor_scalar(u[b][:, :, :], u[b][:, :, :], 2.0, 1.0, ALU.mult, ALU.mult))
                    t.wait()
                    pool.tensor_tensor(u[b][:, :, :], u[b][:, :, :],
                                       beta.unsqueeze(1).to_broadcast([P, JT, D]), ALU.add).then_inc(s_u, 1)
                for b in range(B):
                    s = 2 * i + b
                    rstd(mv1, ve1, rs1, s_mv1, s + 1, s_rs1, t)
                    rstd(mv2, ve2, rs2, s_mv2, s + 1, s_rs2, t)
                assert t.n == 6

            MP = MW // 4
            pieces = [(a * MP, MP) for a in range(4)]

            def fetch(n):
                pool.dma_start(stage[:, :], wpack[n]).then_inc(s_stage, 16)

            def convert(n, w):
                pool.wait_ge(s_stage, 16 * n + 16)
                t = Tally(pool, s_pool2, 12, n)
                for a, m in pieces + [(MW, DW)]:
                    hi = wa[w][:, 0, a:a + m] if a < MW else w3[w][:, 0, :]
                    t.add(pool.tensor_scalar(hi, stage[:, a:a + m], WS, 1.0, ALU.mult, ALU.mult))
                    t.add(pool.tensor_scalar(stage[:, a:a + m], stage[:, a:a + m], WS, 1.0, ALU.mult, ALU.mult))
                t.wait()
                for a, m in pieces:
                    pool.tensor_tensor(wa[w][:, 1, a:a + m], stage[:, a:a + m], wa[w][:, 0, a:a + m], ALU.subtract)
                a, m = MW, FC * D
                t.add(pool.tensor_tensor(w3[w][:, 1, 0:m], stage[:, a:a + m], w3[w][:, 0, 0:m], ALU.subtract))
                t.add(pool.tensor_tensor(w3[w][0:R2, 1, m:DW], stage[0:R2, a + m:a + DW], w3[w][0:R2, 0, m:DW],
                                         ALU.subtract))
                t.wait()
                assert t.n == 12
                pool.sem_inc(s_wset, 1)

            fetch(0)
            convert(0, SH)
            fetch(1)
            convert(1, 0)
            fetch(2)
            convert(2, 1)
            fetch(3)

            pool.wait_ge(s_ycopy, 2 * NI)
            pool.wait_ge(s_place, 1)
            for k in range(K):
                for n in range(NT):
                    pool.indirect_dma_start(
                        out=xs, out_offset=bass.IndirectOffsetOnAxis(ap=place[:, k, n:n + 1], axis=0),
                        in_=y[:, n, :], in_offset=None).then_inc(s_scat[k], 16)
                if k == 0:
                    pool.wait_ge(s_padat, 1)
                    for e in range(E):
                        for j in range(JB):
                            pool.indirect_dma_start(
                                out=xs, out_offset=bass.IndirectOffsetOnAxis(ap=pad_at[:, e, j:j + 1], axis=0),
                                in_=zeros[:, :], in_offset=None, bounds_check=NR * TB - 1, oob_is_err=False)\
                                .then_inc(s_pads, 16)

            pool.wait_ge(s_blocks, 1)

            def after(e):
                n, before = block_range(pool, e)
                return pool.snap(before + n)

            t3 = Tally(pool, s_pool3)
            turn = [0]

            def gather(k, n):
                q = turn[0] % GS
                if turn[0] >= GS:
                    pool.wait_ge(s_sum, turn[0] - GS + 1)
                pool.indirect_dma_start(
                    out=back[q][:, :], out_offset=None, in_=eo,
                    in_offset=bass.IndirectOffsetOnAxis(ap=place[:, k, n:n + 1], axis=0)).then_inc(s_back[q], 16)
                turn[0] += 1

            def add_rows(k, n, m):
                q = m % GS
                pool.wait_ge(s_back[q], 16 * (m // GS + 1))
                t3.add(pool.tensor_scalar(back[q][:, :], back[q][:, :], wk[:, n, k:k + 1], 1.0, ALU.mult, ALU.mult))
                t3.wait()
                base = y if k == 0 and n >= T1 else acc
                pool.tensor_tensor(acc[:, n, :], base[:, n, :], back[q][:, :], ALU.add).then_inc(s_sum, 1)

            def combine(k):
                order = list(range(NT)) if k < K - 1 else list(range(T1, NT)) + list(range(T1))
                for a, n in enumerate(order):
                    gather(k, n)
                    if a >= GS - 1:
                        add_rows(k, order[a - GS + 1], turn[0] - GS)
                for a in range(NT - GS + 1, NT):
                    add_rows(k, order[a], turn[0] - NT + a)

            pool.wait_ge(s_wk, 1)
            for e in range(E):
                done = after(e)
                if e + 2 < E:
                    counted(pool, s_w3, done + S1)
                    convert(e + 3, e % 2)
                    if e + 4 <= E:
                        fetch(e + 4)
                if e >= E - K:
                    counted(pool, s_eo, done * 16 + 16)
                    combine(e - (E - K))

        @block.scalar
        def _(act):
            act.wait_ge(s_halfbd, 1)

            def acts(i, b):
                s = 2 * i + b
                if not isinstance(i, int):
                    act.wait_ge(s_scan, 2 * s - 2)
                for m in range(KD):
                    act.wait_ge(s_mm, 4 * s + 2 * m + 1)
                    act.activation(dec[b][:, m, :], psA[:, 2 * m, :], ACT.Tanh, bias=half_bd[:, m:m + 1], scale=0.5)\
                        .then_inc(s_mmfree, 1)
                    act.wait_ge(s_mm, 4 * s + 2 * m + 2)
                    act.activation(inj[b][:, m, :], psA[:, 2 * m + 1, :], ACT.Identity, bias=bi[:, m:m + 1])\
                        .then_inc(s_mmfree, 1)

            def high(i, b):
                s = 2 * i + b
                act.wait_ge(s_yt, s + 1)
                act.activation(yh[:, :, :], psC[:, :, :], ACT.Copy, scale=XS).then_inc(s_yhi, 1)
                act.activation(y[:, bass.ds(b * (NT // B) + i * JT, JT), :], yb[b][:, :, :], ACT.Copy)\
                    .then_inc(s_ycopy, 1)

            acts(0, 0)
            acts(0, 1)
            with act.Fori(1, NI) as i:
                acts(i, 0)
                high(i - 1, 0)
                acts(i, 1)
                high(i - 1, 1)
            high(NI - 1, 0)
            high(NI - 1, 1)

            act.wait_ge(s_e4, 1)
            act.activation(ex[:, :, :], ex[:, :, :], ACT.Exp).then_inc(s_exp, 1)
            act.activation(sil[:, 0, 0:2], half_bd[:, :], ACT.Silu).then_inc(s_act, 1)
            act.wait_ge(s_act, 1)

            def split_x(b):
                act.wait_ge(s_xtr, b + 1)
                act.activation(xb[:, 0, :, :].rearrange("p k t -> p (k t)"), psC[:, PO, :], ACT.Copy, scale=XS)\
                    .then_inc(s_xhi, 1)

            def ffn_block(g, nxt=True, mid=None):
                def silu(c):
                    act.wait_ge(s_hv, NC * g + c + 1)
                    act.wait_ge(s_g32, NC * g + c + 1 - SLOTS + HVS)
                    n = P if c < FC else REM
                    act.activation(sil[0:n, c % SLOTS, :] if c < FC else sil[R2:R2 + n, c % SLOTS, :],
                                   psA[0:n, c % HVS, 0:TB], ACT.Silu, scale=1.0 / (XS * WS)).then_inc(s_sil, 1)

                def high(c):
                    act.wait_ge(s_g32, NC * g + c + 1 + HVS)
                    n = P if c < FC else REM
                    act.activation(g_hi[0:n, c, :], g32[0:n, c % SLOTS, :], ACT.Copy).then_inc(s_ghi, 1)

                for c in range(NC):
                    silu(c)
                    if c:
                        high(c - 1)
                    if c == 2 and mid:
                        mid()
                if nxt:
                    split_x(g + 1)
                high(NC - 1)

            def expert_rows(e, w, n, before):
                with act.Fori(0, n) as i:
                    r = nc.s_assert_within(act.snap(before + i), 0, NR - 1)
                    g = r + S1
                    ffn_block(g)
                    act.wait_ge(s_w3, g + 1)
                    act.wait_ge(s_eo, 16 * r + 16)
                    act.activation(eb[:, :, :], psB[:, :, 0:D], ACT.Copy).then_inc(s_of, 1)
                    act.wait_ge(s_of, g + 2)
                    act.dma_start(eo[bass.ds(r * TB, TB), :].rearrange("(j p) d -> p j d", p=P), eb[:, :, :])\
                        .then_inc(s_eo, 16)

            split_x(0)
            with act.Fori(0, S1) as g:
                ffn_block(g)
            act.wait_ge(s_fill, 16 * NI)
            act.wait_ge(s_blocks, 1)
            experts(act, expert_rows)
            r = all_blocks(act)

            def store(pair, n):
                act.wait_ge(s_fin, n)
                act.dma_start(out[bass.ds(pair * TB, TB), :].rearrange("(j p) d -> p j d", p=P),
                              acc[:, bass.ds(pair * JB, JB), :]).then_inc(s_out, 16)

            def stores(i):
                store(S1 + i - 1, X2 + 2 * (i - X2) - 1)
                store(i - 1 - X2, X2 + 2 * (i - X2))

            ffn_block(r + S1)
            with act.Fori(1, X2 + 1) as i:
                ffn_block(r + S1 + i, mid=lambda: store(S1 + i - 1, i))
            with act.Fori(X2 + 1, S2 - 1) as i:
                ffn_block(r + S1 + i, mid=lambda: stores(i))
            i = S2 - 1
            ffn_block(r + S1 + i, nxt=False, mid=lambda: stores(i))
            store(NS - 1, X2 + 2 * (S2 - X2) - 1)
            store(S1 - 1, X2 + 2 * (S2 - X2))
            act.wait_ge(s_out, 16 * NS)

        @block.tensor
        def _(pe):
            pe.wait_ge(s_small, 16)
            pe.wait_ge(s_const, NCONST)

            def first(s):
                return isinstance(s, int) and s == 0

            def products(i, b):
                s = 2 * i + b
                pe.wait_ge(s_xt[b], 16 * i + 16)
                for m in range(KD):
                    for w in range(2):
                        q = 2 * m + w
                        if not first(s):
                            pe.wait_ge(s_mmfree, 4 * s + q - 3)
                        for k in range(KD):
                            last = pe.matmul(psA[:, q, :], wdi[:, w, k, m * P:(m + 1) * P], xt[b][:, k, :],
                                             start=(k == 0), stop=(k == KD - 1))
                        last.then_inc(s_mm, 1)

            def states(i, b):
                s = 2 * i + b
                pe.wait_ge(s_scan, 2 * s + 2)
                for h in range(2):
                    if not first(s):
                        pe.wait_ge(s_zfree, 2 * s + h - 1)
                    for j in range(2):
                        for m in range(KD):
                            t0 = (2 * h + j) * P
                            last = pe.transpose(psB[:, h, j * D + m * P:j * D + (m + 1) * P],
                                                st[b][:, m, t0:t0 + P], ident[:, :])
                    last.then_inc(s_st, 1)

            def y_turn(i, b):
                s = 2 * i + b
                pe.wait_ge(s_yb, s + 1)
                if not first(s):
                    pe.wait_ge(s_gev, s)
                for k in range(KD):
                    for j in range(JT):
                        last = pe.transpose(psC[:, k, j * P:(j + 1) * P], yb[b][:, j, k * P:(k + 1) * P], ident[:, :])
                last.then_inc(s_yt, 1)

            def gates(i, b):
                s = 2 * i + b
                pe.wait_ge(s_ylo, s + 1)
                parts = [(yh, gw_hi), (yh, gw_lo), (yl, gw_hi)]
                for j in range(JT):
                    for n, (a, w) in enumerate(parts):
                        for k in range(KD):
                            last = pe.matmul(psC[:, 0, j * E:(j + 1) * E], a[:, k, j * P:(j + 1) * P], w[:, k, :],
                                             start=(n == 0 and k == 0), stop=(n == 2 and k == KD - 1))
                last.then_inc(s_gate, 1)

            pe.wait_ge(s_gwh, 2)
            products(0, 0)
            products(0, 1)
            states(0, 0)
            states(0, 1)
            with pe.Fori(1, NI) as i:
                products(i, 0)
                y_turn(i - 1, 0)
                products(i, 1)
                gates(i - 1, 0)
                y_turn(i - 1, 1)
                states(i, 0)
                gates(i - 1, 1)
                states(i, 1)
            for b in range(B):
                y_turn(NI - 1, b)
                gates(NI - 1, b)

            pe.wait_ge(s_mask, 1)
            m = mask_h[:, :, :].rearrange("p t e -> p (t e)")
            pe.matmul(psC[:, 1, 0:NT * E], tri[:, :], m, start=True, stop=True)
            pe.matmul(psC[:, 1, NT * E:2 * NT * E], ones[:, :], m, start=True, stop=True).then_inc(s_rank, 1)

            def turn_rows(b):
                pe.wait_ge(s_rows, 16 * b + 16)
                for k in range(KD):
                    for j in range(JB):
                        last = pe.transpose(psC[:, PO, k * TB + j * P:k * TB + (j + 1) * P],
                                            rows[:, j, k * P:(k + 1) * P], ident[:, :])
                last.then_inc(s_xtr, 1)

            def ffn_block(w, g, nxt=True):
                pe.wait_ge(s_x, g + 1)
                W = wa[w][:, :, :].rearrange("p s (k c n) -> p s k c n", k=KD, n=P)
                W3 = w3[w][:, :, :].rearrange("p s (c d) -> p s c d", d=D)

                def side(dst, ci):
                    for k in range(KD):
                        for n, (ws, xs_) in enumerate([(0, 0), (0, 1), (1, 0)]):
                            last = pe.matmul(dst, W[:, ws, k, ci, :], xb[:, xs_, k, :],
                                             start=(k == 0 and n == 0), stop=(k == KD - 1 and n == 2))
                    return last

                for c in range(NC):
                    before = c - 4 if c >= 4 else (c + 4 if c + 4 < NC else c) - NC
                    pe.wait_ge(s_g32, NC * g + before + 1 + HVS)
                    last = side(psA[:, c % HVS, 0:TB], 2 * c)
                    if c < FC:
                        last = side(psA[:, c % HVS, TB:2 * TB], 2 * c + 1)
                    last.then_inc(s_hv, 1)
                    if c == 2 and nxt:
                        turn_rows(g + 1)
                pe.wait_ge(s_of, g + 1)
                for c in range(NC):
                    pe.wait_ge(s_g, NC * g + c + 1 + SLOTS)
                    for j in range(JB):
                        o = psB[:, j, 0:D]
                        if c < FC:
                            for n, (a, ws) in enumerate([(g_hi, 0), (g_hi, 1), (g_lo, 0)]):
                                pe.matmul(o, a[:, c, j * P:(j + 1) * P], W3[:, ws, c, :],
                                          start=(c == 0 and n == 0), stop=False)
                        else:
                            r = R2 + REM
                            for ws in range(2):
                                last = pe.matmul(o, g_hi[0:r, c, j * P:(j + 1) * P], W3[0:r, ws, c, :],
                                                 start=False, stop=(ws == 1))
                last.then_inc(s_w3, 1)

            turn_rows(0)
            pe.wait_ge(s_wset, 1)
            with pe.Fori(0, S1) as g:
                ffn_block(SH, g)

            def expert(e, w, n, before):
                counted(pe, s_wset, e + 2)
                with pe.Fori(0, n) as i:
                    ffn_block(w, before + i + S1)

            pe.wait_ge(s_blocks, 1)
            experts(pe, expert)
            r = all_blocks(pe)
            with pe.Fori(S1, NS - 1) as i:
                ffn_block(SH, r + i)
            ffn_block(SH, r + NS - 1, nxt=False)

        @block.vector
        def _(dve):
            dve.wait_ge(s_small, 16)
            dve.wait_ge(s_const, NCONST)
            dve.tensor_scalar(half_bd[:, :], sm[:, OC:OC + 2], 0.5, None, ALU.mult).then_inc(s_halfbd, 1)
            dve.tensor_scalar(gw_hi[:, :, :].rearrange("p k e -> p (k e)"), wg, WS, None, ALU.mult).then_inc(s_gwh, 1)
            dve.wait_ge(s_gwh, 1)
            dve.scalar_tensor_tensor(gw_lo[:, :, :].rearrange("p k e -> p (k e)"), wg, WS,
                                     gw_hi[:, :, :].rearrange("p k e -> p (k e)"), ALU.mult, ALU.subtract)\
                .then_inc(s_gwh, 1)

            def scans(i, b, t):
                s = 2 * i + b
                dve.wait_ge(s_mmfree, 4 * s + 4)
                t.add(dve.tensor_scalar(dec[b][:, :, :], dec[b][:, :, :], 0.5, 0.5, ALU.mult, ALU.add))
                t.wait()
                if not isinstance(i, int):
                    dve.wait_ge(s_st, 2 * s - 2)
                for m in range(KD):
                    dve.tensor_tensor_scan(st[b][:, m, :], dec[b][:, m, :], inj[b][:, m, :], carry[:, b, m:m + 1],
                                           ALU.mult, ALU.add).then_inc(s_scan, 1)
                dve.wait_ge(s_scan, 2 * s + 2)
                t.add(dve.tensor_copy(carry[:, b, :], st[b][:, :, TT - 1]))

            def norms(i, b, t):
                s = 2 * i + b
                for j in range(JT):
                    if j % 2 == 0:
                        dve.wait_ge(s_st, 2 * s + j // 2 + 1)
                    ins = dve.bn_stats(stat[:, j, :], psB[:, j // 2, (j % 2) * D:(j % 2 + 1) * D])
                t.add(ins)
                t.wait()
                dve.sem_inc(s_passed, 1)
                for j in range(JT):
                    ins = dve.bn_aggr(mv1[:, j, :], stat[:, j, :])
                ins.then_inc(s_mv1, 1)
                dve.wait_ge(s_mv1, s + 1)
                for j in range(JT):
                    ins = dve.scalar_tensor_tensor(zr[:, j, :], psB[:, j // 2, (j % 2) * D:(j % 2 + 1) * D],
                                                   mv1[:, j, 0:1], gamma, ALU.subtract, ALU.mult)
                    if j % 2:
                        ins.then_inc(s_zfree, 1)
                dve.wait_ge(s_zfree, 2 * s + 2)
                dve.wait_ge(s_rs1, s + 1)
                dve.wait_ge(s_u, s + 1)
                for j in range(JT):
                    ins = dve.scalar_tensor_tensor(zr[:, j, :], zr[:, j, :], rs1[:, j:j + 1], u[b][:, j, :],
                                                   ALU.mult, ALU.add)
                ins.then_inc(s_r, 1)
                dve.wait_ge(s_r, s + 1)
                for j in range(JT):
                    ins = dve.bn_stats(stat[:, j, :], zr[:, j, :])
                t.add(ins)
                t.wait()
                dve.sem_inc(s_passed, 1)
                for j in range(JT):
                    ins = dve.bn_aggr(mv2[:, j, :], stat[:, j, :])
                ins.then_inc(s_mv2, 1)
                dve.wait_ge(s_rs2, s + 1)
                if not isinstance(i, int):
                    dve.wait_ge(s_ycopy, s - 1)
                for j in range(JT):
                    ins = dve.tensor_scalar(yb[b][:, j, :], zr[:, j, :], mv2[:, j, 0:1], rs2[:, j:j + 1],
                                            ALU.subtract, ALU.mult)
                ins.then_inc(s_yb, 1)

            def low(i, b):
                s = 2 * i + b
                dve.wait_ge(s_yhi, s + 1)
                for k in range(KD):
                    ins = dve.scalar_tensor_tensor(yl[:, k, :], psC[:, k, :], XS, yh[:, k, :], ALU.mult, ALU.subtract)
                ins.then_inc(s_ylo, 1)

            def logits(i, b):
                s = 2 * i + b
                dve.wait_ge(s_gate, s + 1)
                dve.scalar_tensor_tensor(gate[:, bass.ds(b * (NT // B) + i * JT, JT), :],
                                         psC[:, 0, 0:JT * E].rearrange("p (t e) -> p t e", e=E), 1.0 / (XS * WS),
                                         rb.unsqueeze(1).to_broadcast([P, JT, E]), ALU.mult, ALU.add)\
                    .then_inc(s_gev, 1)

            t = Tally(dve, s_dve)
            scans(0, 0, t)
            scans(0, 1, t)
            norms(0, 0, t)
            norms(0, 1, t)
            PER = t.n
            with dve.Fori(1, NI) as i:
                t = Tally(dve, s_dve, PER, i)
                scans(i, 0, t)
                low(i - 1, 0)
                scans(i, 1, t)
                logits(i - 1, 0)
                low(i - 1, 1)
                norms(i, 0, t)
                logits(i - 1, 1)
                norms(i, 1, t)
                assert t.n == PER
            for b in range(B):
                low(NI - 1, b)
                logits(NI - 1, b)

            t = Tally(dve, s_route)

            def te(ap):
                return ap.unsqueeze(1).to_broadcast([P, NT, E])

            dve.wait_ge(s_gev, 2 * NI)
            for n in range(NT):
                ins = dve.max(top[:, n, :], gate[:, n, :])
            t.add(ins)
            t.wait()
            dve.tensor_tensor(ex[:, :, :], gate[:, :, :], top[:, :, 0:1].to_broadcast([P, NT, E]), ALU.subtract)\
                .then_inc(s_e4, 1)
            for n in range(NT):
                ins = dve.max_index(topi[:, n, :], top[:, n, :], gate[:, n, :])
            t.add(ins)
            t.wait()
            t.add(dve.tensor_copy(topf[:, :, :], topi[:, :, 0:K]))
            t.wait()
            tek = hot.rearrange("p (t e k) -> p t e k", e=E, k=K)
            t.add(dve.tensor_tensor(tek, te(iota_e[:, :]).unsqueeze(3).to_broadcast([P, NT, E, K]),
                                    topf[:, :, :].unsqueeze(2).to_broadcast([P, NT, E, K]), ALU.is_equal))
            t.wait()
            t.add(dve.reduce_sum(mask[:, :, :], tek, axis=AX_X))
            t.wait()
            dve.tensor_copy(mask_h[:, :, :], mask[:, :, :]).then_inc(s_mask, 1)
            dve.wait_ge(s_exp, 1)
            t.add(dve.tensor_tensor(ex[:, :, :], ex[:, :, :], mask[:, :, :], ALU.mult))
            t.wait()
            t.add(dve.reduce_sum(es[:, :], ex[:, :, :], axis=AX_X))
            t.wait()
            t.add(dve.reciprocal(es[:, :], es[:, :]))
            dve.wait_ge(s_rank, 1)
            t.add(dve.tensor_copy(tot[:, :, :], psC[:, 1, NT * E:2 * NT * E].rearrange("p (t e) -> p e t", e=E)))
            t.wait()
            flat = "p e t -> p (e t)"
            t.add(dve.tensor_tensor_scan(inc[:, :, :].rearrange(flat), seg[:, :, :].rearrange(flat),
                                         tot[:, :, :].rearrange(flat), 0.0, ALU.mult, ALU.add))
            t.wait()
            t.add(dve.tensor_scalar(cnt_i[:, 0, :], inc[:, :, NT - 1], 1.0, TB - 1.0, ALU.mult, ALU.add))
            t.wait()
            t.add(dve.tensor_single_scalar(cnt_i[:, 1, :], cnt_i[:, 0, :], TB.bit_length() - 1,
                                           ALU.logical_shift_right))
            t.wait()
            nblk, upto, start, limit, tail = (cnt[:, n, :] for n in range(5))
            t.add(dve.tensor_scalar(nblk, cnt_i[:, 1, :], 1.0, None, ALU.max))
            t.wait()
            t.add(dve.tensor_tensor_scan(upto, one8[:, :], nblk, 0.0, ALU.mult, ALU.add))
            t.add(dve.tensor_copy(blocks[:, 0, :], nblk))
            t.wait()
            t.add(dve.tensor_tensor(start, upto, nblk, ALU.subtract))
            t.wait()
            dve.tensor_copy(blocks[:, 1, :], start).then_inc(s_blocks, 1)
            t.add(dve.tensor_tensor(inc[:, :, :], inc[:, :, :], tot[:, :, :], ALU.subtract))
            t.add(dve.scalar_tensor_tensor(tail, start, float(TB), cnt_i[:, 0, :], ALU.mult, ALU.add))
            t.wait()
            t.add(dve.scalar_tensor_tensor(inc[:, :, :], start.unsqueeze(2).to_broadcast([P, E, NT]), float(TB),
                                           inc[:, :, :], ALU.mult, ALU.add))
            t.wait()
            t.add(dve.tensor_tensor(key[:, :, :], psC[:, 1, 0:NT * E].rearrange("p (t e) -> p t e", e=E),
                                    inc[:, :, :].rearrange("p e t -> p t e"), ALU.add))
            t.wait()
            t.add(dve.tensor_scalar(key[:, :, :], key[:, :, :], -1.0, BIG, ALU.mult, ALU.add))
            t.wait()
            t.add(dve.tensor_tensor(key[:, :, :], key[:, :, :], mask[:, :, :], ALU.mult))
            t.wait()
            for n in range(NT):
                ins = dve.max(top[:, n, :], key[:, n, :])
            t.add(ins)
            t.wait()
            dve.tensor_scalar(place[:, :, :], top[:, :, 0:K].rearrange("p t k -> p k t"), -1.0, BIG,
                              ALU.mult, ALU.add).then_inc(s_place, 1)
            t.add(dve.tensor_scalar(limit, upto, float(TB), None, ALU.mult))
            t.add(dve.tensor_tensor(pad[:, :, :], tail.unsqueeze(2).to_broadcast([P, E, JB]),
                                    iota_r[:, :].unsqueeze(1).to_broadcast([P, E, JB]), ALU.add))
            t.wait()
            t.add(dve.tensor_scalar(pad[:, :, :], pad[:, :, :], 1.0 - TB, None, ALU.add))
            t.wait()
            t.add(dve.tensor_tensor(pad2[:, :, :], pad[:, :, :], limit.unsqueeze(2).to_broadcast([P, E, JB]),
                                    ALU.is_ge))
            t.wait()
            dve.scalar_tensor_tensor(pad_at[:, :, :], pad2[:, :, :], BIG, pad[:, :, :], ALU.mult, ALU.add)\
                .then_inc(s_padat, 1)
            t.add(dve.scalar_tensor_tensor(ex[:, :, :], ex[:, :, :], 1.0 / WS,
                                           es[:, :].unsqueeze(2).to_broadcast([P, NT, E]), ALU.mult, ALU.mult))
            tke = hot.rearrange("p (t k e) -> p t k e", e=E, k=K)
            tke2 = hot2.rearrange("p (t k e) -> p t k e", e=E, k=K)
            t.add(dve.tensor_tensor(tke, key[:, :, :].unsqueeze(2).to_broadcast([P, NT, K, E]),
                                    top[:, :, 0:K].unsqueeze(3).to_broadcast([P, NT, K, E]), ALU.is_equal))
            t.wait()
            t.add(dve.tensor_tensor(tke2, tke, ex[:, :, :].unsqueeze(2).to_broadcast([P, NT, K, E]), ALU.mult))
            t.wait()
            dve.reduce_sum(wk[:, :, :], tke2, axis=AX_X).then_inc(s_wk, 1)

            def split_x(b):
                dve.wait_ge(s_xhi, b + 1)
                dve.scalar_tensor_tensor(xb[:, 1, :, :].rearrange("p k t -> p (k t)"), psC[:, PO, :], XS,
                                         xb[:, 0, :, :].rearrange("p k t -> p (k t)"), ALU.mult, ALU.subtract)\
                    .then_inc(s_x, 1)

            def ffn_block(g, nxt=True):
                def gated(c):
                    dve.wait_ge(s_g, NC * g + c + 1)
                    dve.wait_ge(s_sil, NC * g + c + 1)
                    r0, n = (0, P) if c < FC else (R2, REM)
                    src = psA[:, c % HVS, TB:2 * TB] if c < FC else psA[R2:R2 + REM, c % HVS, 0:TB]
                    dve.scalar_tensor_tensor(g32[0:n, c % SLOTS, :], src, 1.0 / (XS * WS),
                                             sil[r0:r0 + n, c % SLOTS, :], ALU.mult, ALU.mult).then_inc(s_g32, 1)

                def low(c):
                    dve.wait_ge(s_ghi, NC * g + c + 1)
                    if c < FC:
                        dst, n = g_lo[:, c, :], P
                    else:
                        dst, n = g_hi[R2:R2 + REM, c, :], REM
                    dve.tensor_tensor(dst, g32[0:n, c % SLOTS, :], g_hi[0:n, c, :], ALU.subtract).then_inc(s_g, 1)

                for c in range(NC):
                    gated(c)
                    if c:
                        low(c - 1)
                low(NC - 1)
                if nxt:
                    split_x(g + 1)

            def add_shared(g, i, to):
                dve.wait_ge(s_w3, g + 1)
                for j in range(JB):
                    n = i * JB + j
                    ins = dve.scalar_tensor_tensor(one(acc, n), psB[:, j, 0:D], 1.0 / WS, one(to, n), ALU.mult, ALU.add)
                ins.then_inc(s_of, 1)

            split_x(0)
            with dve.Fori(0, S1) as g:
                ffn_block(g)
                add_shared(g, g, y)

            def expert_rows(e, w, n, before):
                with dve.Fori(0, n) as i:
                    ffn_block(before + i + S1)

            dve.wait_ge(s_blocks, 1)
            experts(dve, expert_rows)
            r = all_blocks(dve)

            NOPS = 14

            def finish(pair, n):
                t = Tally(dve, s_norm, NOPS, n - 1)
                for j in range(JB):
                    ins = dve.bn_stats(stat[:, j, :], one(acc, pair * JB + j))
                t.add(ins)
                t.wait()
                dve.sem_inc(s_passed, 1)
                for j in range(JB):
                    ins = dve.bn_aggr(mv1[:, j, :], stat[:, j, :])
                t.add(ins)
                t.wait()
                t.add(dve.tensor_scalar(nv[:, :], mv1[:, 0:JB, 1], LN_EPS, None, ALU.add))
                t.wait()
                t.add(dve.tensor_single_scalar(na[:, :].bitcast(I32), nv[:, :].bitcast(I32), 1,
                                               ALU.logical_shift_right))
                t.wait()
                t.add(dve.tensor_scalar(nr[:, :].bitcast(I32), na[:, :].bitcast(I32), -1.0, float(0x5f3759df),
                                        ALU.mult, ALU.add))
                for _ in range(3):
                    t.wait()
                    t.add(dve.tensor_tensor(na[:, :], nr[:, :], nr[:, :], ALU.mult))
                    t.wait()
                    t.add(dve.scalar_tensor_tensor(na[:, :], na[:, :], -0.5, nv[:, :], ALU.mult, ALU.mult))
                    t.wait()
                    t.add(dve.scalar_tensor_tensor(nr[:, :], na[:, :], 1.5, nr[:, :], ALU.add, ALU.mult))
                t.wait()
                for j in range(JB):
                    a = one(acc, pair * JB + j)
                    ins = dve.tensor_scalar(a, a, mv1[:, j, 0:1], nr[:, j:j + 1], ALU.subtract, ALU.mult)
                ins.then_inc(s_fin, 1)
                assert t.n == NOPS

            SUMS = (K - 1) * NT

            def own(i, n, nxt=True):
                g = r + S1 + i
                ffn_block(g, nxt)
                dve.wait_ge(s_sum, SUMS + JB * i + JB)
                add_shared(g, S1 + i, acc)
                counted(dve, s_of, g + 2)
                finish(S1 + i, n)

            def other(i, n):
                counted(dve, s_sum, SUMS + JB * S2 + JB * i + JB)
                finish(i, n)

            with dve.Fori(0, X2) as i:
                own(i, i + 1)
            with dve.Fori(X2, S2 - 1) as i:
                own(i, X2 + 2 * (i - X2) + 1)
                other(i - X2, X2 + 2 * (i - X2) + 2)
            own(S2 - 1, X2 + 2 * (S2 - 1 - X2) + 1, nxt=False)
            other(S1 - 1, X2 + 2 * (S2 - 1 - X2) + 2)


def pack(a):
    x = np.asarray(a["L0_attn_x"])
    B, T, D = x.shape
    x_tok = np.ascontiguousarray(x.reshape(B * T, D))
    xT = np.ascontiguousarray(x_tok.T.reshape(D // P, P, B * T).transpose(1, 0, 2))

    def cols(v):
        return np.asarray(v).reshape(D // P, P).T

    def rows(m):
        m = np.asarray(m)
        return m.reshape(D // P, P, -1).transpose(1, 0, 2).reshape(P, -1)

    small = np.concatenate(
        [np.broadcast_to(np.asarray(a[f"L0_attn_{n}"])[None], (P, D)) for n in ("gamma", "beta")]
        + [np.broadcast_to(np.asarray(a["L0_ffn_routing_bias"])[None], (P, a["L0_ffn_routing_bias"].shape[0]))]
        + [cols(a["L0_attn_bd"]), cols(a["L0_attn_bi"]), rows(np.asarray(a["L0_ffn_Wg"]).T)]
        + [rows(a["L0_attn_Wd"]), rows(a["L0_attn_Wi"])], axis=1)

    W1 = np.concatenate([np.asarray(a["L0_ffn_Ws1"])[None], np.asarray(a["L0_ffn_W1"])])
    W2 = np.concatenate([np.asarray(a["L0_ffn_Ws2"])[None], np.asarray(a["L0_ffn_W2"])])
    W3 = np.concatenate([np.asarray(a["L0_ffn_Ws3"])[None], np.asarray(a["L0_ffn_W3"])])
    E1, H, _ = W1.shape
    FC, REM, KD = dims(H, D)
    up = np.zeros((E1, P, KD, 2 * FC + 1, P), W1.dtype)
    for n, w in enumerate((W1, W2)):
        wt = w.transpose(0, 2, 1).reshape(E1, KD, P, H).transpose(0, 2, 1, 3)
        up[:, :, :, n:2 * FC:2, :] = wt[..., :FC * P].reshape(E1, P, KD, FC, P)
        up[:, :, :, 2 * FC, n * 64:n * 64 + REM] = wt[..., FC * P:]
    down = np.zeros((E1, P, FC + 1, D), W3.dtype)
    w3t = W3.transpose(0, 2, 1)
    down[:, :, :FC] = w3t[:, :FC * P].reshape(E1, FC, P, D).transpose(0, 2, 1, 3)
    for n in range(2):
        down[:, n * 64:n * 64 + REM, FC] = w3t[:, FC * P:]
    wpack = np.concatenate([up.reshape(E1, P, -1), down.reshape(E1, P, -1)], axis=2)
    return {"xT": xT, "x_tok": x_tok, "small": np.ascontiguousarray(small), "wpack": np.ascontiguousarray(wpack)}


def kernel(**inputs):
    import concourse.bacc as bacc
    from concourse.bass_utils import run_bass_kernel_spmd

    arrays = pack(inputs)
    nc = bacc.Bacc("TRN2", target_bir_lowering=False, num_devices=1)
    args = [nc.dram_tensor(n, v.shape, mybir.dt.from_np(v.dtype), kind="ExternalInput").ap()
            for n, v in arrays.items()]
    out = nc.dram_tensor("out", arrays["x_tok"].shape, F32, kind="ExternalOutput").ap()
    build(nc, *args, out)
    r = run_bass_kernel_spmd(nc, [arrays], core_ids=[0])
    return r.results[0]["out"].reshape(inputs["L0_attn_x"].shape)
```

```python
from contextlib import ExitStack

import numpy as np
import concourse.bass as bass
from concourse import mybir

P = 128
ALU = mybir.AluOpType
ACT = mybir.ActivationFunctionType
F32 = mybir.dt.float32
F16 = mybir.dt.float16
U32 = mybir.dt.uint32
AX_X = mybir.AxisListType.X
I32 = mybir.dt.int32
LN_EPS = 1e-5

TT = 512
JT = TT // P
TB = 256
JB = TB // P
XS = 16.0
WS = 64.0


def dims(H, D):
    full = H // P
    rem = H - full * P
    return full, rem, D // P


class Tally:

    def __init__(self, eng, sem, per_turn=0, turn=0):
        self.eng, self.sem, self.base, self.n = eng, sem, turn * per_turn, 0

    def add(self, ins):
        self.n += 1
        return ins.then_inc(self.sem, 1)

    def wait(self):
        self.eng.wait_ge(self.sem, self.base + self.n)


def build(nc, xT, x_tok, small, wpack, out):
    E1 = wpack.shape[0]
    E = E1 - 1
    K = 4
    N, D = x_tok.shape
    B = 2
    H = 682
    FC, REM, KD = dims(H, D)
    NC = FC + 1
    NT = N // P
    NSTEP = N // TT
    AHEAD = 2
    EARLY = NSTEP - AHEAD
    NS = N // TB
    S1 = 9
    S2 = NS - S1
    NR = K * N // TB + E
    MW = KD * (2 * FC + 1) * P
    DW = NC * D
    HVS = 4
    SLOTS = 3
    GS = 4
    FIELD_BITS = 7
    FIELD = 1 << FIELD_BITS
    R2 = 64
    BIG = 32768.0
    OG, OB, OR, OC, OGW = 0, D, 2 * D, 2 * D + E, 2 * D + E + 4
    OW = OGW + KD * E
    SM = OW + 2 * KD * D
    NG = K * N // P + E
    assert small.shape[1] == SM and KD == 2 and B == 2 and JB == 2 and NG * P < BIG
    assert HVS == 4 and NC == 6
    assert NT < FIELD and NR < FIELD and (NG + 1) * FIELD ** 2 < 1 << 24
    OWN = [[], [0, 1], [2], [3], [4], [], [5, 6]]
    EXTRA = [0, 2, 2, 3, 2, 0, 0]
    assert OWN[-1]
    assert len(EXTRA) == S2 and sum(EXTRA) == S1 and sorted(sum(OWN, [])) == list(range(S2))

    eo = nc.dram_tensor("rows_by_place", [NG * P, D], F32, kind="Internal").ap()
    xs = eo.bitcast(F16)

    ctx = ExitStack()
    with ctx:
        def sb(name, shape, dt):
            return ctx.enter_context(nc.sbuf_tensor(name, shape, dt))

        def sem(name):
            return ctx.enter_context(nc.semaphore(name))

        sm = sb("sm", [P, SM], F32)
        ident = sb("ident", [P, P], F32)
        tri = sb("tri", [P, P], F16)
        ones = sb("ones", [P, P], F16)
        zeros = sb("zeros", [P, D], F32)
        y = sb("y", [P, NT, D], F32)
        y_hl = sb("y_hl", [P, NT, 2, D], F16)
        work = sb("work", [P, 15, KD * TT], F32)

        def kt(n):
            return work[:, n, :].rearrange("p (k t) -> p k t", k=KD)

        def jd(n):
            return work[:, n, :].rearrange("p (j d) -> p j d", j=JT)

        xt, dec, inj, st, u, zr, yb = ([v(2 * n + b) for b in range(B)]
                                       for n, v in enumerate((kt, kt, kt, kt, jd, jd, jd)))
        yT = kt(14)
        hot = work[:, 10, :]
        hot2 = work[:, 11, :]
        SETW = (MW + DW) // (KD * TT) + 1
        assert 2 * SETW <= 10
        ident_h = sb("ident_h", [P, P], F16)
        neg_half = sb("neg_half", [P, JT], F32)
        carry = sb("carry", [P, B, KD], F32)
        stat = sb("stat", [P, 8, 6], F32)
        mv1 = [sb(f"mv1{b}", [P, JT, 2], F32) for b in range(B)]
        mv2 = [sb(f"mv2{b}", [P, JT, 2], F32) for b in range(B)]
        ve = sb("ve", [P, JT], F32)
        rs1 = [sb(f"rs1{b}", [P, JT], F32) for b in range(B)]
        rs2 = [sb(f"rs2{b}", [P, JT], F32) for b in range(B)]

        gate = sb("gate", [P, NT, E], F32)
        top = sb("top", [P, NT, 8], F32)
        topi = sb("topi", [P, NT, 8], U32)
        topf = sb("topf", [P, NT, K], F32)
        ex = sb("ex", [P, NT, E], F32)
        es = sb("es", [P, NT], F32)
        iota_e = sb("iota_e", [P, E], F32)
        iota_r = sb("iota_r", [P, 1], F32)
        mask = sb("mask", [P, NT, E], F32)
        mask_h = sb("mask_h", [P, NT, E], F16)
        seg = sb("seg", [P, E, NT], F32)
        tot = sb("tot", [P, E, NT], F32)
        inc = sb("inc", [P, E, NT], F32)
        key = sb("key", [P, NT, E], F32)
        wk = sb("wk", [P, NT, K], F32)
        place = sb("place", [P, K, NT], U32)
        one8 = sb("one8", [P, E], F32)
        cnt = sb("cnt", [P, 8, E], F32)
        cnt_i = sb("cnt_i", [P, 3, E], I32)
        pair_n = sb("pair_n", [P, E // 2], F32)
        blocks = sb("blocks", [P, E], I32)
        pairs = sb("pairs", [P, E // 2], I32)
        pad = sb("pad", [P, E], F32)
        pad2 = sb("pad2", [P, E], F32)
        pad_at = sb("pad_at", [P, E], U32)

        stage = sb("stage", [P, MW + DW], F32)
        wshared = sb("wshared", [P, 2 * (MW + DW)], F16)

        def weight_set(flat):
            return (flat[:, 0:2 * MW].rearrange("p (s n) -> p s n", s=2),
                    flat[:, 2 * MW:2 * (MW + DW)].rearrange("p (s n) -> p s n", s=2))

        wa, w3 = zip(*[weight_set(f) for f in
                       [work[:, w * SETW:(w + 1) * SETW, :].rearrange("p n f -> p (n f)").bitcast(F16)
                        for w in range(2)] + [wshared]])
        SH = 2
        rows = sb("rows", [P, JB, 2 * D], F16)
        xb = sb("xb", [P, 2, KD, TB], F16)
        sil = sb("sil", [P, SLOTS, TB], F32)
        g32 = sb("g32", [P, SLOTS, TB], F32)
        g_hi = sb("g_hi", [P, NC, TB], F16)
        g_lo = sb("g_lo", [P, FC, TB], F16)
        eb = sb("eb", [P, JB, D], F32)
        back = sb("back", [P, GS, D], F32)
        low_room = back
        assert GS == JT
        nmv = sb("nmv", [P, 8, 2], F32)
        nv = sb("nv", [P, 8], F32)
        nr = sb("nr", [P, 8], F32)
        na = sb("na", [P, 8], F32)
        nb = sb("nb", [P, 8], F32)

        psA = ctx.enter_context(nc.psum_tensor("psA", [P, 4, 512], F32))
        psB = ctx.enter_context(nc.psum_tensor("psB", [P, 2, 512], F32))
        psC = ctx.enter_context(nc.psum_tensor("psC", [P, 2, 512], F32))
        PO = 0

        small_loaded = sem("small_loaded")
        wdi_loaded = sem("wdi_loaded")
        passed = sem("passed")
        xT_loaded = [sem(f"xT_loaded{b}") for b in range(B)]
        x_loaded = [sem(f"x_loaded{b}") for b in range(B)]
        weights_loaded = sem("weights_loaded")
        bases_written = sem("bases_written")
        consts_ready = sem("consts_ready")
        pool_steps = sem("pool_steps")
        convert_steps = sem("convert_steps")
        scale_steps = sem("scale_steps")
        products_ready = sem("products_ready")
        products_read = sem("products_read")
        table_loaded = sem("table_loaded")
        dve_steps = sem("dve_steps")
        states_ready = sem("states_ready")
        states_turned = sem("states_turned")
        states_read = sem("states_read")
        moments1_ready = sem("moments1_ready")
        moments2_ready = sem("moments2_ready")
        rstd1_ready = sem("rstd1_ready")
        rstd2_ready = sem("rstd2_ready")
        residual_ready = sem("residual_ready")
        first_normed = sem("first_normed")
        y_ready = sem("y_ready")
        y_copied = sem("y_copied")
        y_high_ready = sem("y_high_ready")
        y_low_ready = sem("y_low_ready")
        y_scaled = sem("y_scaled")
        x_doubled = sem("x_doubled")
        yT_ready = sem("yT_ready")
        yT_turned = sem("yT_turned")
        logits_summed = sem("logits_summed")
        logits_ready = sem("logits_ready")
        shifted_ready = sem("shifted_ready")
        exps_ready = sem("exps_ready")
        route_steps = sem("route_steps")
        mask_ready = sem("mask_ready")
        ranks_ready = sem("ranks_ready")
        blocks_ready = sem("blocks_ready")
        places_ready = sem("places_ready")
        pad_places_ready = sem("pad_places_ready")
        row_weights_ready = sem("row_weights_ready")
        scattered = [sem(f"scattered{k}") for k in range(K)]
        pads_written = [sem(f"pads_written{n}") for n in range(2)]
        weight_set_ready = sem("weight_set_ready")
        up_weights_ready = sem("up_weights_ready")
        rows_loaded = sem("rows_loaded")
        spare_filled = sem("spare_filled")
        rows_turned = sem("rows_turned")
        xb_ready = sem("xb_ready")
        up_ready = sem("up_ready")
        silu_ready = sem("silu_ready")
        gated_ready = sem("gated_ready")
        gated_high_ready = sem("gated_high_ready")
        gated_low_ready = sem("gated_low_ready")
        down_ready = sem("down_ready")
        down_read = sem("down_read")
        rows_stored = sem("rows_stored")
        rows_gathered = [sem(f"rows_gathered{q}") for q in range(GS)]
        rows_added = sem("rows_added")
        lot_ready = sem("lot_ready")
        norm_steps = sem("norm_steps")
        groups_normed = sem("groups_normed")
        out_stored = sem("out_stored")

        block = ctx.enter_context(nc.Block())

        gamma = sm[:, OG:OG + D]
        beta = sm[:, OB:OB + D]
        rb = sm[:, OR:OR + E]
        bd = sm[:, OC:OC + 2]
        bi = sm[:, OC + 2:OC + 4]
        wg = sm[:, OGW:OGW + KD * E]
        wdi = sm[:, OW:OW + 2 * KD * D].rearrange("p (w k e) -> p w k e", w=2, k=KD)
        NCONST = 13

        steps = range(NSTEP)

        def tok(s):
            return (s % B) * (N // B) + s // B * TT

        def counted(eng, sem_, value):
            eng.wait_ge(sem_, value)
            eng.sem_inc(passed, 1)

        def one(ap, t):
            return ap[:, bass.ds(t, 1), :].rearrange("p a d -> p (a d)")

        moves_rows = (nc.sync, nc.scalar)

        def expert_row(eng, e):
            word = eng.value_load(blocks[0:1, bass.ds(e, 1)], min_val=1, max_val=(NG + 1) * FIELD ** 2 - 1)
            groups = eng.snap(word & (FIELD - 1), min_val=1, max_val=NT)
            first = eng.snap((word >> FIELD_BITS) & (FIELD - 1), min_val=0, max_val=NR)
            group = eng.snap(word >> (2 * FIELD_BITS), min_val=0, max_val=NG) if eng in moves_rows else None
            return eng.snap(groups >> 1), eng.snap(groups & 1), first, group

        def pair_rows(eng, p):
            if eng in moves_rows:
                return [expert_row(eng, 2 * p + w) for w in range(2)]
            word = eng.value_load(pairs[0:1, bass.ds(p, 1)], min_val=1, max_val=(NT + 1) * FIELD ** 2 - 1)
            first = eng.snap(word & (FIELD - 1), min_val=0, max_val=NR)
            n = [eng.snap((word >> FIELD_BITS) & (FIELD - 1), min_val=1, max_val=NT),
                 eng.snap(word >> (2 * FIELD_BITS), min_val=1, max_val=NT)]
            return [(eng.snap(n[0] >> 1), eng.snap(n[0] & 1), first, None),
                    (eng.snap(n[1] >> 1), eng.snap(n[1] & 1), eng.snap(first + ((n[0] + 1) >> 1)), None)]

        def expert_blocks(eng, row, run):
            full, half, first, group = row
            with eng.If(full > 0):
                with eng.Fori(0, full) as i:
                    run(TB, first + i, None if group is None else group + JB * i)
            with eng.If(half > 0):
                run(P, eng.snap(first + full), None if group is None else eng.snap(group + JB * full))

        def blocks_until(eng, e):
            full, half, first, _ = expert_row(eng, e)
            return eng.snap(eng.snap(first + full) + half)

        FINISH = [[S1 + q for q in OWN[i]] + list(range(sum(EXTRA[:i]), sum(EXTRA[:i + 1]))) for i in range(S2)]
        LOTS = [i for i in range(S2) if FINISH[i]]
        ORDER = []
        for i in range(S2):
            ORDER += [q for q in dict.fromkeys([S1 + i] + FINISH[i]) if q not in ORDER]
        assert sorted(ORDER) == list(range(NS))

        def experts(eng, run, first=None):
            with eng.Fori(0, E // 2) as p:
                pair = pair_rows(eng, p)
                for w in range(2):
                    if first:
                        first(2 * p + w)
                    expert_blocks(eng, pair[w], lambda T, b, group: run(w, T, b, group))

        @block.sync
        def _(sp):
            sp.dma_start(sm[:, OW:SM], small[:, OW:SM]).then_inc(wdi_loaded, 16)

            spare = K * N
            def fill_spare():
                sp.wait_ge(consts_ready, NCONST)
                sp.dma_start(eo[spare:NG * P, :].rearrange("(n p) d -> p n d", p=P),
                             zeros[:, :].unsqueeze(1).to_broadcast([P, NG - spare // P, D])).then_inc(spare_filled, 16)

            def load_shared(b, i):
                if not isinstance(b, int) or b > 0:
                    sp.wait_ge(rows_turned, b)
                sp.dma_start(rows[:, :, :], y_hl[:, bass.ds(JB * i, JB), :, :].rearrange("p j s d -> p j (s d)"))\
                    .then_inc(rows_loaded, 16)

            def load_turned(s):
                if s >= B:
                    sp.wait_ge(products_ready, 4 * (s - B) + 4)
                sp.dma_start(xt[s % B], xT[:, :, tok(s):tok(s) + TT]).then_inc(xT_loaded[s % B], 16)

            def load_residual(s):
                if s >= B:
                    sp.wait_ge(first_normed, s - B + 1)
                sp.dma_start(u[s % B], x_tok[tok(s):tok(s) + TT, :].rearrange("(j p) d -> p j d", p=P))\
                    .then_inc(x_loaded[s % B], 16)

            load_turned(0)
            sp.dma_start(sm[:, 0:OW], small[:, 0:OW]).then_inc(small_loaded, 16)
            load_turned(1)
            load_residual(0)
            load_residual(1)
            load_turned(2)
            for s in steps:
                if B <= s + 1 < NSTEP:
                    load_residual(s + 1)
                if s + AHEAD + 1 < NSTEP:
                    load_turned(s + AHEAD + 1)
                if s == 1:
                    fill_spare()
                if s == EARLY:
                    load_shared(0, 0)

            sp.wait_ge(y_low_ready, NSTEP)
            with sp.Fori(1, S1) as i:
                load_shared(i, i)

            sp.wait_ge(blocks_ready, 1)

            def load_rows(T, b, group):
                sp.wait_ge(rows_turned, S1 + b)
                r0 = nc.s_assert_within(sp.snap(group * P), 0, (NG - T // P) * P)
                sp.dma_start(rows[:, 0:T // P, :], xs[bass.ds(r0, T), :].rearrange("(j p) d -> p j d", p=P))\
                    .then_inc(rows_loaded, 16)

            for e in range(E):
                if e < K:
                    sp.wait_ge(scattered[e], 16 * NT)
                if e < 2:
                    sp.wait_ge(pads_written[e], 16 * (E - 1 if e else 1))
                expert_blocks(sp, expert_row(sp, e), load_rows)
            r = blocks_until(sp, E - 1)
            with sp.Fori(S1, NS) as i:
                load_shared(r + i, i)

        @block.gpsimd
        def _(pool):
            pool.memset(ident[:, :], 0.0).then_inc(bases_written, 1)
            pool.memset(tri[:, :], 1.0).then_inc(bases_written, 1)
            pool.memset(ident_h[:, :], 0.0).then_inc(bases_written, 1)
            pool.memset(seg[:, :, :], 1.0).then_inc(bases_written, 1)
            pool.wait_ge(bases_written, 4)
            pool.affine_select(out=ident[:, :], in_=ident[:, :], compare_op=ALU.not_equal, fill=1.0, base=0,
                               pattern=[[-1, P]], channel_multiplier=1).then_inc(consts_ready, 1)
            pool.affine_select(out=ident_h[:, :], in_=ident_h[:, :], compare_op=ALU.not_equal, fill=1.0, base=0,
                               pattern=[[-1, P]], channel_multiplier=1).then_inc(consts_ready, 1)
            pool.affine_select(out=tri[:, :], in_=tri[:, :], compare_op=ALU.is_gt, fill=0.0, base=0,
                               pattern=[[1, P]], channel_multiplier=-1).then_inc(consts_ready, 1)
            pool.memset(seg[:, :, 0:1], 0.0).then_inc(consts_ready, 1)
            pool.memset(ones[:, :], 1.0).then_inc(consts_ready, 1)
            pool.memset(one8[:, :], 1.0).then_inc(consts_ready, 1)
            pool.memset(zeros[:, :], 0.0).then_inc(consts_ready, 1)
            pool.memset(neg_half[:, :], -0.5).then_inc(consts_ready, 1)
            pool.memset(carry[:, :, :], 0.0).then_inc(consts_ready, 1)
            pool.memset(g_hi[:, :, :], 0.0).then_inc(consts_ready, 1)
            pool.memset(w3[SH][:, 1, FC * D:DW], 0.0).then_inc(consts_ready, 1)
            pool.iota(iota_e[:, :], pattern=[[1, E]], base=0, channel_multiplier=0,
                      allow_small_or_imprecise_dtypes=True).then_inc(consts_ready, 1)
            pool.iota(iota_r[:, :], pattern=[[P, 1]], base=0, channel_multiplier=1,
                      allow_small_or_imprecise_dtypes=True).then_inc(consts_ready, 1)
            pool.sem_inc(down_read, 1)
            pool.sem_inc(gated_ready, HVS)
            pool.sem_inc(gated_low_ready, SLOTS)
            pool.sem_inc(rows_stored, 16)
            pool.wait_ge(small_loaded, 16)
            pool.wait_ge(consts_ready, NCONST)

            t = Tally(pool, pool_steps)

            def rstd(mv, rs, mv_sem, s, rs_sem):
                pool.wait_ge(mv_sem, s + 1)
                t.add(pool.tensor_scalar(ve[:, :], mv[:, :, 1], 1.0, LN_EPS, ALU.mult, ALU.add))
                t.wait()
                t.add(pool.tensor_tensor(rs[:, :], ve[:, :], neg_half[:, :], ALU.pow))
                t.wait()
                pool.sem_inc(rs_sem, 1)

            def residual(s):
                b = s % B
                pool.wait_ge(x_doubled, s + 1)
                pool.tensor_tensor(u[b], u[b], beta.unsqueeze(1).to_broadcast([P, JT, D]), ALU.add)\
                    .then_inc(residual_ready, 1)

            def low_rows(s):
                b = s % B
                g0 = tok(s) // P
                pool.wait_ge(y_high_ready, s + 1)
                pool.wait_ge(y_scaled, s + 1)
                pool.tensor_tensor(y_hl[:, g0:g0 + JT, 1, :], low_room[:, :, :], y_hl[:, g0:g0 + JT, 0, :],
                                   ALU.subtract).then_inc(y_low_ready, 1)

            MP = MW // 4
            pieces = [(a * MP, MP) for a in range(4)] + [(MW, DW // 2), (MW + DW // 2, DW // 2)]

            def fetch(n):
                pool.dma_start(stage[:, :], wpack[n]).then_inc(weights_loaded, 16)

            def parts_of(w, a, m):
                return [(wa[w][:, i, a:a + m] if a < MW else w3[w][:, i, a - MW:a - MW + m]) for i in range(2)]

            def high_part(t, w, a, m):
                t.add(pool.tensor_scalar(parts_of(w, a, m)[0], stage[:, a:a + m], WS, 1.0, ALU.mult, ALU.mult))
                t.add(pool.tensor_scalar(stage[:, a:a + m], stage[:, a:a + m], WS, 1.0, ALU.mult, ALU.mult))

            def low_part(t, w, a, m):
                hi, lo = parts_of(w, a, m)
                full = m if a + m < MW + DW else m - D
                t.add(pool.tensor_tensor(lo[:, 0:full], stage[:, a:a + full], hi[:, 0:full], ALU.subtract))
                if full < m:
                    t.wait()
                    t.add(pool.tensor_tensor(lo[0:R2, full:m], stage[0:R2, a + full:a + m], hi[0:R2, full:m],
                                             ALU.subtract))

            residual(0)
            fetch(0)
            for s in steps:
                b = s % B
                rstd(mv1[b], rs1[b], moments1_ready, s, rstd1_ready)
                if s + 1 < NSTEP:
                    residual(s + 1)
                if 1 <= s <= len(pieces):
                    if s == 1:
                        pool.wait_ge(weights_loaded, 16)
                    high_part(t, SH, *pieces[s - 1])
                rstd(mv2[b], rs2[b], moments2_ready, s, rstd2_ready)
                if s:
                    low_rows(s - 1)
                if 1 <= s <= len(pieces):
                    low_part(t, SH, *pieces[s - 1])
                    if s == 4:
                        t.wait()
                        pool.sem_inc(up_weights_ready, 1)
                    if s == len(pieces):
                        t.wait()
                        pool.sem_inc(weight_set_ready, 1)
                        fetch(1)
            low_rows(NSTEP - 1)

            def convert(n, w):
                pool.wait_ge(weights_loaded, 16 * n + 16)
                t = Tally(pool, convert_steps, 3 * len(pieces) + 1, n - 1)
                for a, m in pieces:
                    high_part(t, w, a, m)
                t.wait()
                for a, m in pieces:
                    low_part(t, w, a, m)
                t.wait()
                pool.sem_inc(weight_set_ready, 1)

            pool.wait_ge(products_ready, 4 * NSTEP)
            pool.wait_ge(states_turned, 2 * NSTEP)
            pool.wait_ge(first_normed, NSTEP)
            pool.wait_ge(y_low_ready, NSTEP)
            for w in range(2):
                last = pool.memset(w3[w][:, 1, FC * D:DW], 0.0)
            last.then_inc(consts_ready, 1)
            pool.wait_ge(consts_ready, NCONST + 1)
            convert(1, 0)
            fetch(2)

            pool.wait_ge(places_ready, 1)
            pool.wait_ge(spare_filled, 16)
            for k in range(K):
                for n in range(NT):
                    pool.indirect_dma_start(
                        out=xs, out_offset=bass.IndirectOffsetOnAxis(ap=place[:, k, n:n + 1], axis=0),
                        in_=y_hl[:, n, :, :].rearrange("p s d -> p (s d)"), in_offset=None).then_inc(scattered[k], 16)
                if k < 2:
                    if k == 0:
                        pool.wait_ge(pad_places_ready, 1)
                    for e in ([0], range(1, E))[k]:
                        pool.indirect_dma_start(
                            out=xs, out_offset=bass.IndirectOffsetOnAxis(ap=pad_at[:, e:e + 1], axis=0),
                            in_=zeros[:, :].bitcast(F16), in_offset=None, bounds_check=NG * P - 1, oob_is_err=False)\
                            .then_inc(pads_written[k], 16)
                if k == 1:
                    convert(2, 1)
                    fetch(3)

            pool.wait_ge(blocks_ready, 1)

            t3 = Tally(pool, scale_steps)
            turn = [0]

            def gather(k, n):
                q = turn[0] % GS
                if turn[0] >= GS:
                    pool.wait_ge(rows_added, turn[0] - GS + 1)
                pool.indirect_dma_start(
                    out=back[:, q, :], out_offset=None, in_=eo,
                    in_offset=bass.IndirectOffsetOnAxis(ap=place[:, k, n:n + 1], axis=0)).then_inc(rows_gathered[q], 16)
                turn[0] += 1

            def add_rows(k, n, m):
                q = m % GS
                pool.wait_ge(rows_gathered[q], 16 * (m // GS + 1))
                t3.add(pool.tensor_scalar(back[:, q, :], back[:, q, :], wk[:, n, k:k + 1], 1.0, ALU.mult, ALU.mult))
                t3.wait()
                pool.tensor_tensor(y[:, n, :], y[:, n, :], back[:, q, :], ALU.add).then_inc(rows_added, 1)

            def combine(k):
                order = list(range(NT)) if k < K - 1 else [n for q in ORDER for n in range(q * JB, (q + 1) * JB)]
                for a, n in enumerate(order):
                    gather(k, n)
                    if a >= GS - 1:
                        add_rows(k, order[a - GS + 1], turn[0] - GS)
                for a in range(NT - GS + 1, NT):
                    add_rows(k, order[a], turn[0] - NT + a)

            pool.wait_ge(row_weights_ready, 1)
            for e in range(E):
                done = blocks_until(pool, e)
                if e + 2 < E:
                    counted(pool, down_ready, done + S1)
                    convert(e + 3, e % 2)
                    if e + 4 <= E:
                        fetch(e + 4)
                if e >= E - K:
                    counted(pool, rows_stored, done * 16 + 16)
                    combine(e - (E - K))

        @block.scalar
        def _(act):
            act.wait_ge(small_loaded, 16)

            def acts(s):
                b = s % B
                if s >= B:
                    act.wait_ge(states_ready, 2 * (s - B) + 2)
                for m in range(KD):
                    act.wait_ge(products_ready, 4 * s + 2 * m + 1)
                    act.activation(dec[b][:, m, :], psA[:, 2 * m, :], ACT.Sigmoid, bias=bd[:, m:m + 1])\
                        .then_inc(products_read, 1)
                    act.wait_ge(products_ready, 4 * s + 2 * m + 2)
                    act.activation(inj[b][:, m, :], psA[:, 2 * m + 1, :], ACT.Identity, bias=bi[:, m:m + 1])\
                        .then_inc(products_read, 1)

            def copies(s, rest=True):
                b = s % B
                g0 = tok(s) // P
                act.wait_ge(y_ready, s + 1)
                act.activation(y_hl[:, g0:g0 + JT, 0, :], yb[b], ACT.Copy, scale=XS).then_inc(y_high_ready, 1)
                if s:
                    act.wait_ge(y_low_ready, s)
                act.activation(low_room[:, :, :], yb[b], ACT.Copy, scale=XS).then_inc(y_scaled, 1)
                act.wait_ge(yT_turned, s + 1)
                act.activation(yT, psC[:, :, :], ACT.Copy).then_inc(yT_ready, 1)
                if rest:
                    copy_y(s)

            def copy_y(s):
                g0 = tok(s) // P
                act.activation(y[:, g0:g0 + JT, :], yb[s % B], ACT.Copy).then_inc(y_copied, 1)

            def twice(s):
                act.wait_ge(x_loaded[s % B], 16 * (s // B) + 16)
                act.activation(u[s % B], u[s % B], ACT.Copy, scale=2.0).then_inc(x_doubled, 1)

            for s in range(AHEAD):
                acts(s)
                if s < B:
                    twice(s)
            for s in steps:
                if B <= s + 1 < NSTEP:
                    twice(s + 1)
                if s:
                    copies(s - 1)
                if s + AHEAD < NSTEP:
                    acts(s + AHEAD)
            def ffn_block(g, T=TB, ahead=None, beside=None):
                def silu(c):
                    act.wait_ge(up_ready, NC * g + c + 1)
                    act.wait_ge(gated_ready, NC * g + c + 1 - SLOTS + HVS)
                    n = P if c < FC else REM
                    r0 = 0 if c < FC else R2
                    act.activation(sil[r0:r0 + n, c % SLOTS, 0:T], psA[0:n, c % HVS, 0:T], ACT.Silu,
                                   scale=1.0 / (XS * WS)).then_inc(silu_ready, 1)

                def high(c):
                    act.wait_ge(gated_ready, NC * g + c + 1 + HVS)
                    n = P if c < FC else REM
                    act.activation(g_hi[0:n, c, 0:T], g32[0:n, c % SLOTS, 0:T], ACT.Copy).then_inc(gated_high_ready, 1)

                first = SLOTS if ahead else 1
                for c in range(first):
                    silu(c)
                if ahead:
                    ahead()
                for c in range(first, NC):
                    if beside:
                        beside(c - 1)
                    if ahead:
                        high(c - first)
                        silu(c)
                    else:
                        silu(c)
                        high(c - first)
                for c in range(NC - first, NC):
                    high(c)

            def expert_rows(w, T, b, group):
                ffn_block(b + S1, T)
                act.wait_ge(down_ready, b + S1 + 1)
                act.wait_ge(rows_stored, 16 * b + 16)
                J = T // P
                act.activation(eb[:, 0:J, :], psB[:, 0:J, 0:D], ACT.Copy).then_inc(down_read, 1)
                act.wait_ge(down_read, b + S1 + 2)
                r0 = nc.s_assert_within(act.snap(group * P), 0, (NG - J) * P)
                act.dma_start(eo[bass.ds(r0, T), :].rearrange("(j p) d -> p j d", p=P), eb[:, 0:J, :])\
                    .then_inc(rows_stored, 16)

            ffn_block(0, ahead=lambda: copies(NSTEP - 1, rest=False))
            copy_y(NSTEP - 1)
            ffn_block(1)
            act.wait_ge(shifted_ready, 1)
            act.activation(ex[:, :, :], ex[:, :, :], ACT.Exp).then_inc(exps_ready, 1)
            act.activation(nmv[:, 0, 0:2], bd, ACT.Silu).then_inc(table_loaded, 1)
            act.wait_ge(table_loaded, 1)
            with act.Fori(2, S1) as g:
                ffn_block(g)
            act.wait_ge(blocks_ready, 1)
            experts(act, expert_rows)
            r = blocks_until(act, E - 1)

            stored = [0]

            def norm_groups(lot, part, parts):
                if part == 0:
                    act.wait_ge(lot_ready, lot + 1)
                groups = list(enumerate(q * JB + j for q in FINISH[LOTS[lot]] for j in range(JB)))
                for a, n in groups[part * len(groups) // parts:(part + 1) * len(groups) // parts]:
                    act.activation(y[:, n, :], y[:, n, :], ACT.Identity, scale=nr[:, a:a + 1], bias=nb[:, a:a + 1])\
                        .then_inc(groups_normed, 1)

            def store(lot):
                act.wait_ge(groups_normed, JB * sum(len(FINISH[i]) for i in LOTS[:lot + 1]))
                pairs = FINISH[LOTS[lot]]
                for run in [[q for q in pairs if q >= S1], [q for q in pairs if q < S1]]:
                    if run:
                        q, m = run[0], len(run)
                        act.dma_start(out[q * TB:(q + m) * TB, :].rearrange("(j p) d -> p j d", p=P),
                                      y[:, q * JB:(q + m) * JB, :]).then_inc(out_stored, 16)
                        stored[0] += 1

            for i in range(S2):
                lot = LOTS.index(i - 2) if i - 2 in LOTS else None
                ffn_block(r + S1 + i, beside=None if lot is None else lambda c: norm_groups(lot, c, NC - 1))
                if lot is not None:
                    store(lot)
            for lot in [n for n, i in enumerate(LOTS) if i >= S2 - 2]:
                norm_groups(lot, 0, 1)
                store(lot)
            act.wait_ge(out_stored, 16 * stored[0])

        @block.tensor
        def _(pe):
            pe.wait_ge(wdi_loaded, 16)

            def products(s, ms=range(KD)):
                b = s % B
                pe.wait_ge(xT_loaded[b], 16 * (s // B) + 16)
                for m in ms:
                    for w in range(2):
                        q = 2 * m + w
                        if s:
                            pe.wait_ge(products_read, 4 * (s - 1) + q + 1)
                        for k in range(KD):
                            last = pe.matmul(psA[:, q, :], wdi[:, w, k, m * P:(m + 1) * P], xt[b][:, k, :],
                                             start=(k == 0), stop=(k == KD - 1))
                        last.then_inc(products_ready, 1)

            def states(s):
                b = s % B
                pe.wait_ge(states_ready, 2 * s + 2)
                for h in range(2):
                    if s:
                        pe.wait_ge(states_read, 2 * (s - 1) + h + 1)
                    for j in range(2):
                        for m in range(KD):
                            t0 = (2 * h + j) * P
                            last = pe.transpose(psB[:, h, j * D + m * P:j * D + (m + 1) * P],
                                                st[b][:, m, t0:t0 + P], ident[:, :])
                    last.then_inc(states_turned, 1)

            def y_turned(s):
                b = s % B
                pe.wait_ge(y_ready, s + 1)
                if s:
                    pe.wait_ge(logits_ready, s)
                for k in range(KD):
                    for j in range(JT):
                        last = pe.transpose(psC[:, k, j * P:(j + 1) * P], yb[b][:, j, k * P:(k + 1) * P], ident[:, :])
                last.then_inc(yT_turned, 1)

            def gates(s):
                pe.wait_ge(yT_ready, s + 1)
                for j in range(JT):
                    for k in range(KD):
                        last = pe.matmul(psC[:, 0, j * E:(j + 1) * E], yT[:, k, j * P:(j + 1) * P],
                                         wg[:, k * E:(k + 1) * E], start=(k == 0), stop=(k == KD - 1))
                last.then_inc(logits_summed, 1)

            def ranks():
                pe.wait_ge(mask_ready, 1)
                m = mask_h[:, :, :].rearrange("p t e -> p (t e)")
                pe.matmul(psC[:, 1, 0:NT * E], tri[:, :], m, start=True, stop=True)
                pe.matmul(psC[:, 1, NT * E:2 * NT * E], ones[:, :], m, start=True, stop=True).then_inc(ranks_ready, 1)

            def turn_rows(b, bank=psC[:, PO, :]):
                pe.wait_ge(rows_loaded, 16 * b + 16)
                turned = bank.bitcast(F16)
                for q in range(2 * KD):
                    for j in range(JB):
                        last = pe.transpose(turned[:, q * TB + j * P:q * TB + (j + 1) * P],
                                            rows[:, j, q * P:(q + 1) * P], ident_h[:, :])
                last.then_inc(rows_turned, 1)

            def up(w, g, chunks, T=TB, nxt=False):
                W = wa[w][:, :, :].rearrange("p s (k c n) -> p s k c n", k=KD, n=P)

                def side(dst, ci):
                    for k in range(KD):
                        for n, (ws, xs_) in enumerate([(0, 0), (0, 1), (1, 0)]):
                            last = pe.matmul(dst, W[:, ws, k, ci, :], xb[:, xs_, k, 0:T],
                                             start=(k == 0 and n == 0), stop=(k == KD - 1 and n == 2))
                    return last

                pe.wait_ge(xb_ready, g + 1)
                for c in chunks:
                    before = c - 4 if c >= 4 else (c + 4 if c + 4 < NC else c) - NC
                    pe.wait_ge(gated_ready, NC * g + before + 1 + HVS)
                    last = side(psA[:, c % HVS, 0:T], 2 * c)
                    if c < FC:
                        last = side(psA[:, c % HVS, TB:TB + T], 2 * c + 1)
                    last.then_inc(up_ready, 1)
                    if c == 2 and nxt:
                        turn_rows(g + 1)

            def down(w, g, T=TB):
                W3 = w3[w][:, :, :].rearrange("p s (c d) -> p s c d", d=D)
                pe.wait_ge(down_read, g + 1)
                for c in range(NC):
                    pe.wait_ge(gated_low_ready, NC * g + c + 1 + SLOTS)
                    for j in range(T // P):
                        o = psB[:, j, 0:D]
                        if c < FC:
                            for n, (a, ws) in enumerate([(g_hi, 0), (g_hi, 1), (g_lo, 0)]):
                                pe.matmul(o, a[:, c, j * P:(j + 1) * P], W3[:, ws, c, :],
                                          start=(c == 0 and n == 0), stop=False)
                        else:
                            r = R2 + REM
                            for ws in range(2):
                                last = pe.matmul(o, g_hi[0:r, c, j * P:(j + 1) * P], W3[0:r, ws, c, :],
                                                 start=False, stop=(ws == 1))
                last.then_inc(down_ready, 1)

            def ffn_block(w, g, T=TB, nxt=True):
                up(w, g, range(NC), T, nxt)
                down(w, g, T)

            products(0)
            products(1, [0])
            pe.wait_ge(small_loaded, 16)
            pe.wait_ge(consts_ready, NCONST)
            states(0)
            products(1, [1])
            for s in steps:
                if s:
                    y_turned(s - 1)
                if s == EARLY:
                    pe.wait_ge(products_read, 4 * NSTEP)
                    turn_rows(0, psA[:, HVS - 1, :])
                if s + AHEAD < NSTEP:
                    products(s + AHEAD, [0])
                if s:
                    gates(s - 1)
                if s + AHEAD < NSTEP:
                    products(s + AHEAD, [1])
                if s + 1 < NSTEP:
                    states(s + 1)
                if s == EARLY:
                    pe.wait_ge(up_weights_ready, 1)
                    up(SH, 0, [0, 1])
                if s == EARLY + 1:
                    up(SH, 0, [2, 3])
            y_turned(NSTEP - 1)
            up(SH, 0, [4, 5])
            gates(NSTEP - 1)
            pe.wait_ge(states_read, 2 * NSTEP)
            pe.wait_ge(weight_set_ready, 1)
            down(SH, 0)
            pe.wait_ge(logits_ready, NSTEP)
            turn_rows(1)
            ffn_block(SH, 1)
            ffn_block(SH, 2)
            ranks()
            with pe.Fori(3, S1) as g:
                ffn_block(SH, g)

            pe.wait_ge(blocks_ready, 1)
            experts(pe, lambda w, T, b, group: ffn_block(w, b + S1, T),
                    first=lambda e: counted(pe, weight_set_ready, e + 2))
            r = blocks_until(pe, E - 1)
            with pe.Fori(S1, NS - 1) as i:
                ffn_block(SH, r + i)
            ffn_block(SH, r + NS - 1, nxt=False)

        @block.vector
        def _(dve):
            dve.wait_ge(small_loaded, 16)
            dve.wait_ge(consts_ready, NCONST)
            t = Tally(dve, dve_steps)

            def scan(s, m):
                b = s % B
                dve.wait_ge(products_read, 4 * s + 2 * m + 2)
                if m == 0 and s >= B:
                    dve.wait_ge(states_turned, 2 * (s - B) + 2)
                if m == 0 and s:
                    t.wait()
                dve.tensor_tensor_scan(st[b][:, m, :], dec[b][:, m, :], inj[b][:, m, :], carry[:, b, m:m + 1],
                                       ALU.mult, ALU.add).then_inc(states_ready, 1)
                if m == KD - 1:
                    dve.wait_ge(states_ready, 2 * s + 2)
                    t.add(dve.tensor_copy(carry[:, b, :], st[b][:, :, TT - 1]))

            def first_norm(s):
                b = s % B
                for j in range(JT):
                    if j % 2 == 0:
                        dve.wait_ge(states_turned, 2 * s + j // 2 + 1)
                    ins = dve.bn_stats(stat[:, j, :], psB[:, j // 2, (j % 2) * D:(j % 2 + 1) * D])
                t.add(ins)
                t.wait()
                for j in range(JT):
                    ins = dve.bn_aggr(mv1[b][:, j, :], stat[:, j, :])
                ins.then_inc(moments1_ready, 1)
                dve.wait_ge(moments1_ready, s + 1)
                for j in range(JT):
                    ins = dve.scalar_tensor_tensor(zr[b][:, j, :], psB[:, j // 2, (j % 2) * D:(j % 2 + 1) * D],
                                                   mv1[b][:, j, 0:1], gamma, ALU.subtract, ALU.mult)
                    if j % 2:
                        ins.then_inc(states_read, 1)
                if s + 1 < NSTEP:
                    scan(s + 1, 1)
                dve.wait_ge(states_read, 2 * s + 2)
                dve.wait_ge(rstd1_ready, s + 1)
                dve.wait_ge(residual_ready, s + 1)
                for j in range(JT):
                    ins = dve.scalar_tensor_tensor(zr[b][:, j, :], zr[b][:, j, :], rs1[b][:, j:j + 1], u[b][:, j, :],
                                                   ALU.mult, ALU.add)
                ins.then_inc(first_normed, 1)
                dve.wait_ge(first_normed, s + 1)
                for j in range(JT):
                    ins = dve.bn_stats(stat[:, j, :], zr[b][:, j, :])
                t.add(ins)
                t.wait()
                for j in range(JT):
                    ins = dve.bn_aggr(mv2[b][:, j, :], stat[:, j, :])
                ins.then_inc(moments2_ready, 1)

            def second_norm(s):
                b = s % B
                dve.wait_ge(rstd2_ready, s + 1)
                if s >= B:
                    dve.wait_ge(y_copied, s - B + 1)
                    dve.wait_ge(y_low_ready, s - B + 1)
                for j in range(JT):
                    ins = dve.tensor_scalar(yb[b][:, j, :], zr[b][:, j, :], mv2[b][:, j, 0:1], rs2[b][:, j:j + 1],
                                            ALU.subtract, ALU.mult)
                ins.then_inc(y_ready, 1)

            def logits(s):
                g0 = tok(s) // P
                dve.wait_ge(logits_summed, s + 1)
                dve.tensor_tensor(gate[:, g0:g0 + JT, :], psC[:, 0, 0:JT * E].rearrange("p (t e) -> p t e", e=E),
                                  rb.unsqueeze(1).to_broadcast([P, JT, E]), ALU.add).then_inc(logits_ready, 1)

            def te(ap):
                return ap.unsqueeze(1).to_broadcast([P, NT, E])

            ngroup, nfull, nblock, upto, b_upto, start, limit, tail = (cnt[:, n, :] for n in range(8))
            flat = "p e t -> p (e t)"

            def largest():
                dve.wait_ge(logits_ready, NSTEP)
                for n in range(NT):
                    ins = dve.max(top[:, n, :], gate[:, n, :])
                t.add(ins)
                t.wait()
                dve.tensor_tensor(ex[:, :, :], gate[:, :, :], top[:, :, 0:1].to_broadcast([P, NT, E]), ALU.subtract)\
                    .then_inc(shifted_ready, 1)

            def choose():
                for n in range(NT):
                    ins = dve.max_index(topi[:, n, :], top[:, n, :], gate[:, n, :])
                t.add(ins)
                t.wait()
                t.add(dve.tensor_copy(topf[:, :, :], topi[:, :, 0:K]))
                t.wait()
                tek = hot.rearrange("p (t e k) -> p t e k", e=E, k=K)
                t.add(dve.tensor_tensor(tek, te(iota_e[:, :]).unsqueeze(3).to_broadcast([P, NT, E, K]),
                                        topf[:, :, :].unsqueeze(2).to_broadcast([P, NT, E, K]), ALU.is_equal))
                t.wait()
                t.add(dve.reduce_sum(mask[:, :, :], tek, axis=AX_X))
                t.wait()
                dve.tensor_copy(mask_h[:, :, :], mask[:, :, :]).then_inc(mask_ready, 1)

            def count():
                dve.wait_ge(exps_ready, 1)
                t.add(dve.tensor_tensor(ex[:, :, :], ex[:, :, :], mask[:, :, :], ALU.mult))
                t.wait()
                t.add(dve.reduce_sum(es[:, :], ex[:, :, :], axis=AX_X))
                t.wait()
                t.add(dve.reciprocal(es[:, :], es[:, :]))
                dve.wait_ge(ranks_ready, 1)
                t.add(dve.tensor_copy(tot[:, :, :], psC[:, 1, NT * E:2 * NT * E].rearrange("p (t e) -> p e t", e=E)))
                t.wait()
                t.add(dve.tensor_tensor_scan(inc[:, :, :].rearrange(flat), seg[:, :, :].rearrange(flat),
                                             tot[:, :, :].rearrange(flat), 0.0, ALU.mult, ALU.add))
                t.wait()
                t.add(dve.tensor_scalar(cnt_i[:, 0, :], inc[:, :, NT - 1], 1.0, P - 1.0, ALU.mult, ALU.add))
                t.wait()
                t.add(dve.tensor_single_scalar(cnt_i[:, 1, :], cnt_i[:, 0, :], P.bit_length() - 1,
                                               ALU.logical_shift_right))
                t.wait()
                t.add(dve.tensor_scalar(ngroup, cnt_i[:, 1, :], 1.0, None, ALU.max))
                t.wait()
                t.add(dve.tensor_tensor_scan(upto, one8[:, :], ngroup, 0.0, ALU.mult, ALU.add))
                t.add(dve.tensor_copy(cnt_i[:, 2, :], ngroup))
                t.wait()
                t.add(dve.tensor_tensor(start, upto, ngroup, ALU.subtract))
                t.add(dve.tensor_single_scalar(cnt_i[:, 1, :], cnt_i[:, 2, :], 1, ALU.logical_shift_right))
                t.wait()
                t.add(dve.tensor_copy(nfull, cnt_i[:, 1, :]))
                t.wait()
                t.add(dve.tensor_tensor(nblock, ngroup, nfull, ALU.subtract))
                t.wait()
                t.add(dve.tensor_tensor_scan(b_upto, one8[:, :], nblock, 0.0, ALU.mult, ALU.add))
                t.wait()
                t.add(dve.tensor_tensor(b_upto, b_upto, nblock, ALU.subtract))
                t.wait()
                both = ngroup.rearrange("p (q w) -> p q w", w=2)
                t.add(dve.scalar_tensor_tensor(pair_n[:, :], both[:, :, 1], float(FIELD), both[:, :, 0],
                                               ALU.mult, ALU.add))
                t.add(dve.scalar_tensor_tensor(nblock, start, float(FIELD), b_upto, ALU.mult, ALU.add))
                t.wait()
                t.add(dve.scalar_tensor_tensor(pairs[:, :], pair_n[:, :], float(FIELD),
                                               b_upto.rearrange("p (q w) -> p q w", w=2)[:, :, 0],
                                               ALU.mult, ALU.add))
                t.wait()
                dve.scalar_tensor_tensor(blocks[:, :], nblock, float(FIELD), ngroup, ALU.mult, ALU.add)\
                    .then_inc(blocks_ready, 1)

            def places():
                t.add(dve.tensor_tensor(inc[:, :, :], inc[:, :, :], tot[:, :, :], ALU.subtract))
                t.add(dve.scalar_tensor_tensor(tail, start, float(P), cnt_i[:, 0, :], ALU.mult, ALU.add))
                t.wait()
                t.add(dve.scalar_tensor_tensor(inc[:, :, :], start.unsqueeze(2).to_broadcast([P, E, NT]), float(P),
                                               inc[:, :, :], ALU.mult, ALU.add))
                t.wait()
                t.add(dve.tensor_tensor(key[:, :, :], psC[:, 1, 0:NT * E].rearrange("p (t e) -> p t e", e=E),
                                        inc[:, :, :].rearrange("p e t -> p t e"), ALU.add))
                t.wait()
                t.add(dve.tensor_scalar(key[:, :, :], key[:, :, :], -1.0, BIG, ALU.mult, ALU.add))
                t.wait()
                t.add(dve.tensor_tensor(key[:, :, :], key[:, :, :], mask[:, :, :], ALU.mult))
                t.wait()
                for n in range(NT):
                    ins = dve.max(top[:, n, :], key[:, n, :])
                t.add(ins)
                t.wait()
                dve.tensor_scalar(place[:, :, :], top[:, :, 0:K].rearrange("p t k -> p k t"), -1.0, BIG,
                                  ALU.mult, ALU.add).then_inc(places_ready, 1)

            def weights():
                t.add(dve.tensor_scalar(limit, upto, float(P), None, ALU.mult))
                t.add(dve.tensor_tensor(pad[:, :], tail, iota_r[:, :].to_broadcast([P, E]), ALU.add))
                t.wait()
                t.add(dve.tensor_scalar(pad[:, :], pad[:, :], 1.0 - P, None, ALU.add))
                t.wait()
                t.add(dve.tensor_tensor(pad2[:, :], pad[:, :], limit, ALU.is_ge))
                t.wait()
                dve.scalar_tensor_tensor(pad_at[:, :], pad2[:, :], BIG, pad[:, :], ALU.mult, ALU.add)\
                    .then_inc(pad_places_ready, 1)
                t.add(dve.scalar_tensor_tensor(ex[:, :, :], ex[:, :, :], 1.0 / WS,
                                               es[:, :].unsqueeze(2).to_broadcast([P, NT, E]), ALU.mult, ALU.mult))
                tke = hot.rearrange("p (t k e) -> p t k e", e=E, k=K)
                tke2 = hot2.rearrange("p (t k e) -> p t k e", e=E, k=K)
                t.add(dve.tensor_tensor(tke, key[:, :, :].unsqueeze(2).to_broadcast([P, NT, K, E]),
                                        top[:, :, 0:K].unsqueeze(3).to_broadcast([P, NT, K, E]), ALU.is_equal))
                t.wait()
                t.add(dve.tensor_tensor(tke2, tke, ex[:, :, :].unsqueeze(2).to_broadcast([P, NT, K, E]), ALU.mult))
                t.wait()
                dve.reduce_sum(wk[:, :, :], tke2, axis=AX_X).then_inc(row_weights_ready, 1)

            def split_x(b, bank=psC[:, PO, :]):
                dve.wait_ge(rows_turned, b + 1)
                dve.tensor_copy(xb[:, :, :, :].rearrange("p s k t -> p (s k t)"), bank.bitcast(F16))\
                    .then_inc(xb_ready, 1)

            def ffn_block(g, T=TB, nxt=True):
                def gated(c):
                    dve.wait_ge(gated_low_ready, NC * g + c + 1)
                    dve.wait_ge(silu_ready, NC * g + c + 1)
                    r0, n = (0, P) if c < FC else (R2, REM)
                    src = psA[:, c % HVS, TB:TB + T] if c < FC else psA[R2:R2 + REM, c % HVS, 0:T]
                    dve.scalar_tensor_tensor(g32[0:n, c % SLOTS, 0:T], src, 1.0 / (XS * WS),
                                             sil[r0:r0 + n, c % SLOTS, 0:T], ALU.mult, ALU.mult).then_inc(gated_ready, 1)

                def low(c):
                    dve.wait_ge(gated_high_ready, NC * g + c + 1)
                    if c < FC:
                        dst, n = g_lo[:, c, 0:T], P
                    else:
                        dst, n = g_hi[R2:R2 + REM, c, 0:T], REM
                    dve.tensor_tensor(dst, g32[0:n, c % SLOTS, 0:T], g_hi[0:n, c, 0:T], ALU.subtract)\
                        .then_inc(gated_low_ready, 1)

                for c in range(NC):
                    if c == NC - 1 and nxt:
                        dve.wait_ge(up_ready, NC * (g + 1))
                        split_x(g + 1)
                    gated(c)
                    if c:
                        low(c - 1)
                low(NC - 1)

            def add_shared(g, i):
                dve.wait_ge(down_ready, g + 1)
                for j in range(JB):
                    n = i * JB + j
                    ins = dve.scalar_tensor_tensor(one(y, n), psB[:, j, 0:D], 1.0 / WS, one(y, n), ALU.mult, ALU.add)
                ins.then_inc(down_read, 1)

            t = Tally(dve, dve_steps)
            for s, m in ((0, 0), (0, 1), (1, 0)):
                scan(s, m)
            for s in steps:
                first_norm(s)
                if s + 2 < NSTEP:
                    scan(s + 2, 0)
                if s == EARLY:
                    split_x(0, psA[:, HVS - 1, :])
                second_norm(s)
                if s:
                    logits(s - 1)
            ffn_block(0, nxt=False)
            logits(NSTEP - 1)
            split_x(1)
            add_shared(0, 0)
            t = Tally(dve, route_steps)
            for g, part in enumerate((largest, choose, count, places, weights), start=1):
                part()
                ffn_block(g)
                add_shared(g, g)
            with dve.Fori(6, S1) as g:
                ffn_block(g)
                add_shared(g, g)

            dve.wait_ge(blocks_ready, 1)
            experts(dve, lambda w, T, b, group: ffn_block(b + S1, T))
            r = blocks_until(dve, E - 1)

            t = Tally(dve, norm_steps)

            def finish(lot, pairs):
                groups = [y[:, q * JB + j, :] for q in pairs for j in range(JB)]
                m = len(groups)
                if lot:
                    dve.wait_ge(groups_normed, JB * sum(len(FINISH[i]) for i in LOTS[:lot]))
                for j in range(m):
                    ins = dve.bn_stats(stat[:, j, :], groups[j])
                t.add(ins)
                t.wait()
                for j in range(m):
                    ins = dve.bn_aggr(nmv[:, j, :], stat[:, j, :])
                t.add(ins)
                t.wait()
                v, r_, a, mean = nv[:, 0:m], nr[:, 0:m], na[:, 0:m], nmv[:, 0:m, 0]
                t.add(dve.tensor_scalar(v, nmv[:, 0:m, 1], LN_EPS, None, ALU.add))
                t.wait()
                t.add(dve.tensor_single_scalar(a.bitcast(I32), v.bitcast(I32), 1, ALU.logical_shift_right))
                t.wait()
                t.add(dve.tensor_scalar(r_.bitcast(I32), a.bitcast(I32), -1.0, float(0x5f3759df), ALU.mult, ALU.add))
                for _ in range(3):
                    t.wait()
                    t.add(dve.tensor_tensor(a, r_, r_, ALU.mult))
                    t.wait()
                    t.add(dve.scalar_tensor_tensor(a, a, -0.5, v, ALU.mult, ALU.mult))
                    t.wait()
                    t.add(dve.scalar_tensor_tensor(r_, a, 1.5, r_, ALU.add, ALU.mult))
                t.wait()
                dve.scalar_tensor_tensor(nb[:, 0:m], mean, -1.0, r_, ALU.mult, ALU.mult).then_inc(lot_ready, 1)

            summed = (K - 1) * NT
            for i in range(S2):
                g = r + S1 + i
                ffn_block(g, nxt=i < S2 - 1)
                if i - 1 in LOTS:
                    lot = FINISH[i - 1]
                    dve.wait_ge(rows_added, summed + JB * (max(ORDER.index(q) for q in lot) + 1))
                    counted(dve, down_read, g + 1)
                    finish(LOTS.index(i - 1), lot)
                dve.wait_ge(rows_added, summed + JB * (ORDER.index(S1 + i) + 1))
                add_shared(g, S1 + i)
            counted(dve, down_read, g + 2)
            finish(len(LOTS) - 1, FINISH[S2 - 1])


def pack(a):
    x = np.asarray(a["L0_attn_x"])
    B, T, D = x.shape
    x_tok = np.ascontiguousarray(x.reshape(B * T, D))
    xT = np.ascontiguousarray(x_tok.T.reshape(D // P, P, B * T).transpose(1, 0, 2))

    def cols(v):
        return np.asarray(v).reshape(D // P, P).T

    def rows(m):
        m = np.asarray(m)
        return m.reshape(D // P, P, -1).transpose(1, 0, 2).reshape(P, -1)

    small = np.concatenate(
        [np.broadcast_to(np.asarray(a[f"L0_attn_{n}"])[None], (P, D)) for n in ("gamma", "beta")]
        + [np.broadcast_to(np.asarray(a["L0_ffn_routing_bias"])[None], (P, a["L0_ffn_routing_bias"].shape[0]))]
        + [cols(a["L0_attn_bd"]), cols(a["L0_attn_bi"]), rows(np.asarray(a["L0_ffn_Wg"]).T)]
        + [rows(a["L0_attn_Wd"]), rows(a["L0_attn_Wi"])], axis=1)

    W1 = np.concatenate([np.asarray(a["L0_ffn_Ws1"])[None], np.asarray(a["L0_ffn_W1"])])
    W2 = np.concatenate([np.asarray(a["L0_ffn_Ws2"])[None], np.asarray(a["L0_ffn_W2"])])
    W3 = np.concatenate([np.asarray(a["L0_ffn_Ws3"])[None], np.asarray(a["L0_ffn_W3"])])
    E1, H, _ = W1.shape
    FC, REM, KD = dims(H, D)
    up = np.zeros((E1, P, KD, 2 * FC + 1, P), W1.dtype)
    for n, w in enumerate((W1, W2)):
        wt = w.transpose(0, 2, 1).reshape(E1, KD, P, H).transpose(0, 2, 1, 3)
        up[:, :, :, n:2 * FC:2, :] = wt[..., :FC * P].reshape(E1, P, KD, FC, P)
        up[:, :, :, 2 * FC, n * 64:n * 64 + REM] = wt[..., FC * P:]
    down = np.zeros((E1, P, FC + 1, D), W3.dtype)
    w3t = W3.transpose(0, 2, 1)
    down[:, :, :FC] = w3t[:, :FC * P].reshape(E1, FC, P, D).transpose(0, 2, 1, 3)
    for n in range(2):
        down[:, n * 64:n * 64 + REM, FC] = w3t[:, FC * P:]
    wpack = np.concatenate([up.reshape(E1, P, -1), down.reshape(E1, P, -1)], axis=2)
    return {"xT": xT, "x_tok": x_tok, "small": np.ascontiguousarray(small), "wpack": np.ascontiguousarray(wpack)}


def kernel(**inputs):
    import concourse.bacc as bacc
    from concourse.bass_utils import run_bass_kernel_spmd

    arrays = pack(inputs)
    nc = bacc.Bacc("TRN2", target_bir_lowering=False, num_devices=1)
    args = [nc.dram_tensor(n, v.shape, mybir.dt.from_np(v.dtype), kind="ExternalInput").ap()
            for n, v in arrays.items()]
    out = nc.dram_tensor("out", arrays["x_tok"].shape, F32, kind="ExternalOutput").ap()
    build(nc, *args, out)
    r = run_bass_kernel_spmd(nc, [arrays], core_ids=[0])
    return r.results[0]["out"].reshape(inputs["L0_attn_x"].shape)
```
